# Optimizing a Trainium2 kernel written in Bass

```python
import numpy as np
import jax
import jax.numpy as jnp

def _softmax(x, axis=-1):
    return jax.nn.softmax(x, axis=axis)

def _gelu(x):
    return jax.nn.gelu(x, approximate=True)

def _silu(x):
    return jax.nn.silu(x)

def _sigmoid(x):
    return jax.nn.sigmoid(x)

def _layernorm(x, axis=-1, eps=1e-05):
    m = jnp.mean(x, axis=axis, keepdims=True)
    v = jnp.var(x, axis=axis, keepdims=True)
    return (x - m) / jnp.sqrt(v + eps)

def _scatter_add(tgt, idx, src, axis=0):
    return tgt.at[idx].add(src)

def _segment_sum(src, seg, n):
    return jax.ops.segment_sum(src, seg, n)
kernel_name = 'mk_gnn_resnorm_d2_gnn_r8_58814a'

def setup_inputs(seed: int=0):
    np.random.seed(seed)
    _w = jnp.asarray

    def _rec_inputs():
        import jax
        import jax.numpy as jnp
        _gk = jax.random.key(seed)
        x = -0.0001006 + 1 * jax.random.normal(jax.random.fold_in(_gk, 1), (6250, 96), jnp.float32)
        src = jax.random.randint(jax.random.fold_in(_gk, 2), (100000,), 0, 6250, jnp.int32)
        dst = jax.random.randint(jax.random.fold_in(_gk, 3), (100000,), 0, 6250, jnp.int32)
        _o = jnp.argsort(dst, stable=True)
        src = src[_o]
        dst = dst[_o]
        edge_attr_96 = 5.93493e-05 + 1.00006 * jax.random.normal(jax.random.fold_in(_gk, 11), (100000, 96), jnp.float32)
        return (x, src, dst, edge_attr_96)
    x, src, dst, edge_attr_96 = _rec_inputs()

    def _L0_gnn_setup():
        import jax, jax.numpy as jnp
        import numpy as np
        N_NODES = 6250
        N_EDGES = 100000
        NIN = 96
        NOUT = 96
        key = jax.random.key(seed)
        ks = jax.random.split(key, 10)
        s = 1.0 / np.sqrt(NIN)
        so = 1.0 / np.sqrt(NOUT)
        return {'x': jax.random.normal(ks[0], (N_NODES, NIN), dtype=jnp.float32), 'edge_index': jax.random.randint(ks[1], (2, N_EDGES), 0, N_NODES, dtype=jnp.int64), 'edge_attr': jax.random.normal(ks[2], (N_EDGES, NIN), dtype=jnp.float32), 'W_edge': jax.random.uniform(ks[3], (NIN, NIN), jnp.float32, -s, s), 'b_edge': jax.random.uniform(ks[4], (NIN,), jnp.float32, -s, s), 'eps': jnp.zeros((), dtype=jnp.float32), 'W1': jax.random.uniform(ks[5], (NOUT, NIN), jnp.float32, -s, s), 'b1': jax.random.uniform(ks[6], (NOUT,), jnp.float32, -s, s), 'W2': jax.random.uniform(ks[7], (NOUT, NOUT), jnp.float32, -so, so), 'b2': jax.random.uniform(ks[8], (NOUT,), jnp.float32, -so, so)}
    _L0_gnn_all = _L0_gnn_setup()
    _L0_gnn_in = {k: v for k, v in _L0_gnn_all.items() if k in ('W_edge', 'b_edge', 'eps', 'W1', 'b1', 'W2', 'b2')}
    del _L0_gnn_all

    def _L1_gnn_setup():
        import jax, jax.numpy as jnp
        import numpy as np
        N = 6250
        E = 100000
        D_IN = 96
        D_OUT = 96
        ALPHA = 0.5
        key = jax.random.key(seed)
        k1, k2, k3, k4, k5, k6 = jax.random.split(key, 6)
        x = jax.random.normal(k1, (N, D_IN), dtype=jnp.float32)
        edge_index = jax.random.randint(k2, (2, E), 0, N, dtype=jnp.int32)
        s = 1.0 / np.sqrt(D_IN)
        W_sd = jax.random.uniform(k3, (D_OUT, D_IN), jnp.float32, -s, s)
        b_sd = jax.random.uniform(k4, (D_OUT,), jnp.float32, -s, s)
        W_ds = jax.random.uniform(k5, (D_OUT, D_IN), jnp.float32, -s, s)
        b_ds = jax.random.uniform(k6, (D_OUT,), jnp.float32, -s, s)
        return {'x': x, 'W_sd': W_sd, 'b_sd': b_sd, 'W_ds': W_ds, 'b_ds': b_ds, 'edge_index': edge_index}
    _L1_gnn_all = _L1_gnn_setup()
    _L1_gnn_in = {k: v for k, v in _L1_gnn_all.items() if k in ('W_sd', 'b_sd', 'W_ds', 'b_ds')}
    del _L1_gnn_all
    return {'x': x, 'src': src, 'dst': dst, 'edge_attr_96': edge_attr_96, 'L0_gnn_W_edge': _L0_gnn_in['W_edge'], 'L0_gnn_b_edge': _L0_gnn_in['b_edge'], 'L0_gnn_eps': _L0_gnn_in['eps'], 'L0_gnn_W1': _L0_gnn_in['W1'], 'L0_gnn_b1': _L0_gnn_in['b1'], 'L0_gnn_W2': _L0_gnn_in['W2'], 'L0_gnn_b2': _L0_gnn_in['b2'], 'L1_gnn_W_sd': _L1_gnn_in['W_sd'], 'L1_gnn_b_sd': _L1_gnn_in['b_sd'], 'L1_gnn_W_ds': _L1_gnn_in['W_ds'], 'L1_gnn_b_ds': _L1_gnn_in['b_ds']}

def reference(x, src, dst, edge_attr_96, L0_gnn_W_edge, L0_gnn_b_edge, L0_gnn_eps, L0_gnn_W1, L0_gnn_b1, L0_gnn_W2, L0_gnn_b2, L1_gnn_W_sd, L1_gnn_b_sd, L1_gnn_W_ds, L1_gnn_b_ds):
    import jax
    import jax.numpy as jnp

    def _L0_gnn_ref(x, edge_index, edge_attr, W_edge, b_edge, eps, W1, b1, W2, b2):
        import jax, jax.numpy as jnp
        import numpy as np
        N_NODES = 6250
        N_EDGES = 100000
        NIN = 96
        NOUT = 96
        ea = edge_attr @ W_edge.T + b_edge
        src, dst = (edge_index[0], edge_index[1])
        msg = jax.nn.relu(x[src] + ea)
        aggr = jax.ops.segment_sum(msg, dst, num_segments=N_NODES)
        h = (1.0 + eps) * x + aggr
        h = jax.nn.relu(h @ W1.T + b1)
        return h @ W2.T + b2

    def _L1_gnn_ref(x, W_sd, b_sd, W_ds, b_ds, edge_index):
        import jax, jax.numpy as jnp
        import numpy as np
        N = 6250
        E = 100000
        D_IN = 96
        D_OUT = 96
        ALPHA = 0.5
        row, col = (edge_index[0], edge_index[1])
        ones = jnp.ones(row.shape, x.dtype)
        out_deg = jax.ops.segment_sum(ones, row, num_segments=N)
        in_deg = jax.ops.segment_sum(ones, col, num_segments=N)
        out_is = jnp.where(out_deg > 0, jax.lax.rsqrt(out_deg), 0.0)
        in_is = jnp.where(in_deg > 0, jax.lax.rsqrt(in_deg), 0.0)
        val = out_is[row] * in_is[col]
        agg = jax.ops.segment_sum(val[:, None] * x[col], row, num_segments=N)
        agg_t = jax.ops.segment_sum(val[:, None] * x[row], col, num_segments=N)
        return ALPHA * (agg @ W_sd.T + b_sd) + (1.0 - ALPHA) * (agg_t @ W_ds.T + b_ds)
    edge_index = jnp.stack([src, dst])
    x = _layernorm(x + _L0_gnn_ref(x, edge_index, edge_attr_96, L0_gnn_W_edge, L0_gnn_b_edge, L0_gnn_eps, L0_gnn_W1, L0_gnn_b1, L0_gnn_W2, L0_gnn_b2), axis=-1)
    x = _layernorm(x + _L1_gnn_ref(x, L1_gnn_W_sd, L1_gnn_b_sd, L1_gnn_W_ds, L1_gnn_b_ds, edge_index), axis=-1)
    return x

_drawn_inputs = setup_inputs


def setup_inputs(seed=0):
    import zlib

    import numpy as np

    out = dict(_drawn_inputs(seed))
    spreads = {}
    factors = {'L0_gnn_b1': 4.973}
    for name, (base, spread) in spreads.items():
        noise = np.random.default_rng([zlib.crc32(name.encode()), seed]).standard_normal(out[name].shape)
        drawn = base * np.exp(spread * noise) if base else spread * noise
        out[name] = jnp.asarray(drawn.astype(out[name].dtype))
    for name, factor in factors.items():
        out[name] = (out[name] * factor).astype(out[name].dtype)
    return out
```

```python
from contextlib import ExitStack

import concourse.bass as bass
from concourse import mybir

F32, F16, I32 = mybir.dt.float32, mybir.dt.float16, mybir.dt.int32
ALU, ACT, AX = mybir.AluOpType, mybir.ActivationFunctionType, mybir.AxisListType

N, E, D = 6250, 100000, 96
P = 128
B = 125
NB = N // B
HT = 8
CH = -(-E // (2 * HT * P))
TILES = 2 * HT * CH
TC = -(-TILES // P)
TT = TC * P
W = 32
ACCW = N + W + 6
G = 5
NG = N // G
GC = -(-NG // P)
GW = G * NB
PAIRS = 25
STRIPS = NG // (2 * PAIRS)
SW = 2 * B
SCALE = 1024.0
EPS = 1e-5


def bank(ps, name, dt=F32):
    return ps(name, [P, 512 if dt == F32 else 1024], dt)


def hold(eng, carrier, sem, value):
    eng.wait_ge(sem, value)
    eng.sem_inc(carrier, 1)


def gnn(nc, x, xT, dst_te, src_te, dst_et, src_et, src_gather, eaT, weT, w1T, b1, w2T, eps, wsdT, wdsT, bsd, bds, out):
    whole = ExitStack()

    def sb_in(scope):
        return lambda name, shape, dt: scope.enter_context(nc.sbuf_tensor(name, shape, dt))

    def ps_in(scope):
        return lambda name, shape, dt: scope.enter_context(nc.psum_tensor(name, shape, dt))

    def sem(name):
        return whole.enter_context(nc.semaphore(name))

    with whole:
        sb = sb_in(whole)
        carrier = {e: sem(f"carrier_{e}") for e in ("pool", "dve")}
        acc = sb("acc", [D + 1, ACCW], F32)
        X = sb("X", [B, NB, D], F32)
        key_te = sb("key_te", [P, TC, P], F32)
        lo_te = sb("lo_te", [P, TC, P], F32)
        rounds = sb("rounds", [1, 2], I32)
        t0row = sb("t0row", [P, GC * P], F32)
        tneg = sb("tneg", [P, TC], F32)
        iota16 = sb("iota16", [P, B], F16)
        iotaw = sb("iotaw", [P, W], F32)
        keytab = sb("keytab", [P, GW], F16)
        ident = sb("ident", [P, P], F32)
        ident16 = sb("ident16", [P, P], F16)
        odeg = sb("odeg", [B, NB], F32)
        ideg = sb("ideg", [B, NB], F32)
        scl = sb("scl", [B, 2, NB], F32)
        layer0 = ExitStack()
        sb = sb_in(layer0)
        dloc = sb("dloc", [P, TILES], F32)
        hi_et = sb("hi_et", [P, TILES], F16)
        lo_et = sb("lo_et", [P, TILES], F16)
        first = sb("first", [1, TILES], I32)

        with ExitStack() as scope:
            sb, ps = sb_in(scope), ps_in(scope)
            di = sb("di", [P, TT], I32)
            si = sb("si", [P, TT], I32)
            dei = sb("dei", [P, TILES], I32)
            sei = sb("sei", [P, TILES], I32)
            df = sb("df", [P, TC, P], F32)
            sf = sb("sf", [P, TT], F32)
            qi = sb("qi", [P, TT], I32)
            qf = sb("qf", [P, TT], F32)
            rf = sb("rf", [P, TT], F32)
            ge = sb("ge", [P, TT], F32)
            cols = sb("cols", [P, 2 * TC + 2 * GC], F32)
            row = sb("row", [P, (2 * TC + 2 * GC) * P], F32)
            wide = sb("wide", [P, 4, P], F32)
            ones = sb("ones", [P, P], F32)
            up_i = sb("up_i", [P, TT], I32)
            up = sb("up", [P, TT], F32)
            down = sb("down", [P, TT], F32)
            thr_i = sb("thr_i", [P, GC], I32)
            thr = sb("thr", [P, GC], F32)
            thr4 = sb("thr4", [P, GC], F32)
            mask = sb("mask", [P, GC], F32)
            tneg_i = sb("tneg_i", [P, TC], I32)
            key_i = sb("key_i", [P, GW], I32)
            sma = sb("sma", [P, GC], F32)
            smb = sb("smb", [P, GC], F32)
            rnf = sb("rnf", [1, 2], F32)
            rni = sb("rni", [1, 2], I32)
            epsc = sb("epsc", [D, 1], F32)
            eps1 = sb("eps1", [D, 1], F32)
            pr = [ps(f"pr{i}", [P, 4, P], F32) for i in range(8)]
            s_idx, s_te, s_x, s_const, s_id = sem("s_idx"), sem("s_te"), sem("s_x"), sem("s_const"), sem("s_id")
            s_wide, s_row, s_v = sem("s_wide"), sem("s_row"), sem("s_v")

            block = scope.enter_context(nc.Block())

            @block.sync
            def _(sp):
                sp.dma_start(di[:, :], dst_te).then_inc(s_te, 16)
                sp.dma_start(si[:, :], src_te).then_inc(s_te, 16)
                sp.dma_start(dei[:, :], dst_et).then_inc(s_idx, 16)
                sp.dma_start(sei[:, :], src_et).then_inc(s_idx, 16)
                sp.dma_start(epsc[:, :], eps.broadcast_to([D, 1])).then_inc(s_x, 16)
                sp.dma_start(acc[0:D, 0:N], xT).then_inc(s_x, 16)
                xb = x.rearrange("(b p) f -> p b f", p=B)
                sp.dma_start(X[0:112, :, :], xb[0:112, :, :]).then_inc(s_x, 16)
                sp.dma_start(X[112:B, :, :], xb[112:B, :, :]).then_inc(s_x, 16)
                sp.wait_ge(s_x, 64)

            @block.gpsimd
            def _(pool):
                nc.gpsimd.iota(up_i[:, :], pattern=[[1, TT]], base=0, channel_multiplier=0).then_inc(s_const, 1)
                nc.gpsimd.iota(thr_i[:, :], pattern=[[G * P, GC]], base=0, channel_multiplier=G).then_inc(s_const, 1)
                nc.gpsimd.iota(tneg_i[:, :], pattern=[[-P, TC]], base=0, channel_multiplier=-1).then_inc(s_const, 1)
                nc.gpsimd.iota(key_i[:, :], pattern=[[1, NB], [NB, G]], base=1, channel_multiplier=0).then_inc(s_const, 1)
                nc.gpsimd.memset(ones[:, :], 1.0).then_inc(s_const, 1)
                for n, m in enumerate((ident, ident16)):
                    nc.gpsimd.memset(m[:, :], 0.0).then_inc(s_id, 1)
                    pool.wait_ge(s_id, 2 * n + 1)
                    nc.gpsimd.affine_select(out=m[:, :], in_=m[:, :], compare_op=ALU.not_equal, fill=1.0, base=0,
                                            pattern=[[-1, P]], channel_multiplier=1).then_inc(s_id, 1)

            @block.tensor
            def _(pe):
                pe.wait_ge(s_id, 4)
                for k in range(2 * TC + 2 * GC):
                    pe.wait_ge(s_wide, k + 1)
                    nc.tensor.matmul(pr[k // 4 % 8][:, k % 4, :], wide[:, k % 4, :], ident[:, :],
                                     start=True, stop=True).then_inc(s_row, 1)

            @block.vector
            def _(dve):
                made = [0]

                def link(ins):
                    made[0] += 1
                    ins.then_inc(s_v, 1)
                    dve.wait_ge(s_v, made[0])

                def low_high(s, n):
                    q, i, r, g = qf[:, 0:n], qi[:, 0:n], rf[:, 0:n], ge[:, 0:n]
                    link(nc.vector.tensor_scalar(i, s, 1.0 / B, None, ALU.mult))
                    link(nc.vector.tensor_copy(q, i))
                    for cmp, sign in ((ALU.is_ge, 1.0), (ALU.is_lt, -1.0)):
                        link(nc.vector.scalar_tensor_tensor(out=r, in0=q, scalar=-float(B), in1=s, op0=ALU.mult, op1=ALU.add))
                        link(nc.vector.tensor_scalar(g, r, float(B) if sign > 0 else 0.0, sign, cmp, ALU.mult))
                        link(nc.vector.tensor_tensor(q, q, g, ALU.add))
                    link(nc.vector.scalar_tensor_tensor(out=r, in0=q, scalar=-float(B), in1=s, op0=ALU.mult, op1=ALU.add))

                def rows(k0, k1):
                    for k in range(k0, k1):
                        if k >= 4:
                            dve.wait_ge(s_row, k - 3)
                        nc.vector.tensor_scalar(wide[:, k % 4, :], ones[:, :], cols[:, k:k + 1], None, ALU.mult).then_inc(s_wide, 1)
                    dve.wait_ge(s_row, k1)
                    for k in range(k0, k1):
                        link(nc.vector.tensor_copy(row[:, k * P:(k + 1) * P], pr[k // 4 % 8][:, k % 4, :]))

                dve.wait_ge(s_te, 32)
                link(nc.vector.tensor_copy(df[:, :, :].rearrange("p c e -> p (c e)"), di[:, :]))
                link(nc.vector.tensor_copy(sf[:, :], si[:, :]))
                link(nc.vector.tensor_reduce(cols[:, 0:TC], df[:, :, :], AX.X, ALU.min))
                link(nc.vector.tensor_reduce(cols[:, TC:2 * TC], df[:, :, :], AX.X, ALU.max))
                dve.wait_ge(s_const, 5)
                rows(0, 2 * TC)
                tmin, tmax = row[:, 0:TT], row[:, TT:2 * TT]
                low_high(sf[:, :], TT)
                link(nc.vector.scalar_tensor_tensor(out=key_te[:, :, :].rearrange("p c e -> p (c e)"),
                                                    in0=df[:, :, :].rearrange("p c e -> p (c e)"), scalar=float(NB),
                                                    in1=qf[:, :], op0=ALU.mult, op1=ALU.add))
                link(nc.vector.tensor_scalar(key_te[:, :, :], key_te[:, :, :], 1.0, None, ALU.add))
                link(nc.vector.tensor_copy(lo_te[:, :, :].rearrange("p c e -> p (c e)"), rf[:, :]))
                dve.wait_ge(s_idx, 32)
                link(nc.vector.tensor_copy(sf[:, 0:TILES], sei[:, :]))
                low_high(sf[:, 0:TILES], TILES)
                link(nc.vector.tensor_copy(hi_et[:, :], qf[:, 0:TILES]))
                link(nc.vector.tensor_copy(lo_et[:, :], rf[:, 0:TILES]))
                link(nc.vector.tensor_copy(sf[:, 0:TILES], dei[:, :]))
                link(nc.vector.tensor_tensor(dloc[:, :], sf[:, 0:TILES], tmin[:, 0:TILES], ALU.subtract))
                link(nc.vector.tensor_copy(first[:, :], tmin[0:1, 0:TILES]))
                link(nc.vector.tensor_copy(up[:, :], up_i[:, :]))
                link(nc.vector.tensor_copy(iota16[:, :], up_i[:, 0:B]))
                link(nc.vector.tensor_copy(iotaw[:, :], up_i[:, 0:W]))
                link(nc.vector.tensor_copy(keytab[:, :], key_i[:, :]))
                link(nc.vector.tensor_copy(tneg[:, :], tneg_i[:, :]))
                link(nc.vector.tensor_copy(thr[:, :], thr_i[:, :]))
                link(nc.vector.tensor_scalar(thr4[:, :], thr[:, :], float(G - 1), None, ALU.add))
                link(nc.vector.tensor_scalar(mask[:, :], thr[:, :], float(N), None, ALU.is_lt))
                link(nc.vector.tensor_scalar(down[:, :], up[:, :], -1.0, float(TT), ALU.mult, ALU.add))
                link(nc.vector.tensor_scalar(up[:, :], up[:, :], 1.0, None, ALU.add))
                for c in range(GC):
                    link(nc.vector.scalar_tensor_tensor(out=rf[:, :], in0=tmax, scalar=thr[:, c:c + 1], in1=down[:, :],
                                                        op0=ALU.is_ge, op1=ALU.mult))
                    link(nc.vector.tensor_reduce(sma[:, c:c + 1], rf[:, :], AX.X, ALU.max))
                    link(nc.vector.scalar_tensor_tensor(out=qf[:, :], in0=tmin, scalar=thr4[:, c:c + 1], in1=up[:, :],
                                                        op0=ALU.is_le, op1=ALU.mult))
                    link(nc.vector.tensor_reduce(smb[:, c:c + 1], qf[:, :], AX.X, ALU.max))
                link(nc.vector.tensor_scalar(cols[:, 2 * TC:2 * TC + GC], sma[:, :], -1.0, float(TT), ALU.mult, ALU.add))
                link(nc.vector.tensor_tensor(smb[:, :], smb[:, :], sma[:, :], ALU.add))
                link(nc.vector.tensor_scalar(smb[:, :], smb[:, :], float(TT), None, ALU.subtract))
                link(nc.vector.tensor_tensor(cols[:, 2 * TC + GC:], smb[:, :], mask[:, :], ALU.mult))
                rows(2 * TC, 2 * TC + 2 * GC)
                link(nc.vector.tensor_copy(t0row[:, :], row[:, 2 * TT:2 * TT + GC * P]))
                link(nc.vector.tensor_tensor(ge[:, :], tmax, tmin, ALU.subtract))
                link(nc.vector.tensor_reduce(rnf[:, 0:1], ge[0:1, :], AX.X, ALU.max))
                link(nc.vector.tensor_reduce(rnf[:, 1:2], row[0:1, 2 * TT + GC * P:], AX.X, ALU.max))
                link(nc.vector.tensor_scalar(rnf[:, 0:1], rnf[:, 0:1], float(W), None, ALU.add))
                link(nc.vector.tensor_scalar(rnf[:, 1:2], rnf[:, 1:2], 1.0, 2.0, ALU.add, ALU.max))
                link(nc.vector.tensor_copy(rni[:, :], rnf[:, :]))
                link(nc.vector.tensor_scalar(rounds[:, 0:1], rni[:, 0:1], W.bit_length() - 1, None, ALU.arith_shift_right))
                link(nc.vector.tensor_scalar(rounds[:, 1:2], rni[:, 1:2], 1, None, ALU.arith_shift_right))
                dve.wait_ge(s_x, 64)
                link(nc.vector.tensor_scalar(eps1[:, :], epsc[:, :], 1.0, None, ALU.add))
                link(nc.vector.tensor_scalar(acc[0:D, 0:N], acc[0:D, 0:N], eps1[:, :], None, ALU.mult))
                link(nc.vector.memset(acc[0:D, N:ACCW], 0.0))
                link(nc.vector.memset(acc[D:D + 1, :], 0.0))

        CREDIT = 2
        with ExitStack() as scope:
            sb, ps = sb_in(scope), ps_in(scope)
            we = sb("we", [D + 1, D], F32)
            ea = [sb(f"ea{h}", [D + 1, HT * P], F32) for h in range(2)]
            idx = [sb(f"idx{h}", [P, HT], I32) for h in range(2)]
            xg = [sb(f"xg{h}", [P, HT, D], F32) for h in range(2)]
            msg = [sb(f"msg{q}", [P, 4, D + 1], F32) for q in range(2)]
            win = [sb(f"win{q}", [P, 4, W], F32) for q in range(2)]
            lo1 = [sb(f"lo1{q}", [P, 4, B], F16) for q in range(2)]
            hi1 = [sb(f"hi1{q}", [P, 4, NB], F16) for q in range(2)]
            pm = [bank(ps, f"pm{q}")[:, 0:4 * D].rearrange("p (j f) -> p j f", j=4) for q in range(2)]
            pw = [bank(ps, f"pw{q}")[0:D + 1, 0:4 * W].rearrange("p (j w) -> p j w", j=4) for q in range(2)]
            pd = [bank(ps, f"pd{h}")[0:B, 0:NB] for h in range(2)]
            s_we, s_one = sem("s_we"), sem("s_one")
            ea_in = [sem(f"ea_in{h}") for h in range(2)]
            idx_in = [sem(f"idx_in{h}") for h in range(2)]
            xg_in = [sem(f"xg_in{h}") for h in range(2)]
            pre_done = [sem(f"pre_done{q}") for q in range(2)]
            relu_done = [sem(f"relu_done{q}") for q in range(2)]
            hot_done = [sem(f"hot_done{q}") for q in range(2)]
            seg_done = [sem(f"seg_done{q}") for q in range(2)]
            added, s_rnd = sem("added"), sem("s_rnd")
            block = scope.enter_context(nc.Block())

            def count(eng):
                return eng.value_load(rounds[0:1, 0:1], min_val=1, max_val=N)

            @block.sync
            def _(sp):
                sp.dma_start(we[:, :], weT).then_inc(s_we, 16)
                sp.wait_ge(s_one, 2)
                with sp.Fori(0, count(sp)) as r:
                    with sp.Fori(0, CH) as i:
                        n = sp.snap(r * CH + i)
                        for h in range(2):
                            sp.wait_ge(pre_done[1], 2 * n + h - 1 + CREDIT)
                            sp.dma_start(ea[h][0:D, :], eaT[:, bass.ds(i * (2 * HT * P) + h * HT * P, HT * P)]).then_inc(ea_in[h], 16)
                            sp.dma_start(idx[h][:, :], src_gather[bass.ds(i * 2 + h, 1), :, :].rearrange("a p t -> (a p) t")).then_inc(idx_in[h], 16)

            @block.gpsimd
            def _(pool):
                with pool.Fori(0, count(pool)) as r:
                    with pool.Fori(0, CH) as i:
                        n = pool.snap(r * CH + i)
                        for h in range(2):
                            hold(pool, carrier["pool"], idx_in[h], n * 16 + 16)
                            for t in range(HT):
                                nc.gpsimd.indirect_dma_start(out=xg[h][:, t, :], out_offset=None, in_=x[:, :],
                                                             in_offset=bass.IndirectOffsetOnAxis(ap=idx[h][:, t:t + 1], axis=0)
                                                             ).then_inc(xg_in[h], 16)

            @block.tensor
            def _(pe):
                pe.sem_inc(pre_done[1], CREDIT)
                pe.wait_ge(s_we, 16)
                with pe.Fori(0, count(pe)) as r:
                    with pe.Fori(0, CH) as i:
                        n = pe.snap(r * CH + i)
                        for h in range(2):
                            pe.wait_ge(ea_in[h], n * 16 + 16)
                            pe.wait_ge(xg_in[h], n * (16 * HT) + 16 * HT)
                            for q in range(2):
                                for j in range(4):
                                    t = 4 * q + j
                                    nc.tensor.matmul(pm[q][:, j, :], ea[h][:, t * P:(t + 1) * P], we[:, :], start=True, stop=False)
                                    last = nc.tensor.matmul(pm[q][:, j, :], ident[:, :], xg[h][:, t, :], start=False, stop=True)
                                last.then_inc(pre_done[q], 1)
                                pe.wait_ge(relu_done[q], 2 * n + h + 1)
                                pe.wait_ge(hot_done[q], 2 * n + h + 1)
                                for j in range(4):
                                    nc.tensor.matmul(pw[q][:, j, :], msg[q][:, j, :], win[q][:, j, :], start=True, stop=True)
                                for j in range(4):
                                    last = nc.tensor.matmul(pd[h][:, :], lo1[q][:, j, :], hi1[q][:, j, :],
                                                            start=(q == 0 and j == 0), stop=(q == 1 and j == 3))
                                last.then_inc(seg_done[q], 1)

            @block.scalar
            def _(act):
                with act.Fori(0, count(act)) as r:
                    with act.Fori(0, CH) as i:
                        n = act.snap(r * CH + i)
                        for h in range(2):
                            for q in range(2):
                                act.wait_ge(pre_done[q], 2 * n + h + 1 + (CREDIT if q else 0))
                                nc.scalar.activation(msg[q][:, :, 0:D], pm[q][:, :, :], ACT.Relu).then_inc(relu_done[q], 1)

            @block.vector
            def _(dve):
                for h in range(2):
                    nc.vector.memset(ea[h][D:D + 1, :], 1.0).then_inc(s_one, 1)
                for q in range(2):
                    nc.vector.memset(msg[q][:, :, D:D + 1], 1.0)
                regs = [dve.alloc_register(f"first_node{k}") for k in range(2 * HT)]
                with dve.Fori(0, count(dve)) as r:
                    nc.vector.memset(odeg[:, :], 0.0).then_inc(s_rnd, 1)
                    hold(dve, carrier["dve"], s_rnd, r * 3 + 1)
                    with dve.Fori(0, CH) as i:
                        n = dve.snap(r * CH + i)
                        dve.load(regs, first[0:1, bass.ds(i * (2 * HT), 2 * HT)])
                        node = [dve.snap(g, min_val=0, max_val=N) for g in regs]
                        for h in range(2):
                            for q in range(2):
                                t0 = i * (2 * HT) + (h * HT + 4 * q)
                                for table, ruler, hot, w in ((dloc, iotaw, win, W), (lo_et, iota16, lo1, B), (hi_et, iota16, hi1, NB)):
                                    last = nc.vector.tensor_tensor(
                                        hot[q][:, :, :], ruler[:, 0:w].unsqueeze(1).broadcast_to([P, 4, w]),
                                        table[:, bass.ds(t0, 4)].unsqueeze(2).broadcast_to([P, 4, w]), ALU.is_equal)
                                last.then_inc(hot_done[q], 1)
                                dve.wait_ge(seg_done[q], 2 * n + h + 1)
                                for j in range(4):
                                    k = h * HT + 4 * q + j
                                    a = acc[:, bass.ds(node[k], W)]
                                    nc.vector.tensor_tensor(a, a, pw[q][:, j, :], ALU.add).then_inc(added, 1)
                                    dve.wait_ge(added, n * 18 + (k + 1 + h))
                            nc.vector.tensor_tensor(odeg[:, :], odeg[:, :], pd[h][:, :], ALU.add).then_inc(added, 1)
                            hold(dve, carrier["dve"], added, n * 18 + 9 * (h + 1))
                    nc.vector.tensor_scalar(dloc[:, :], dloc[:, :], float(W), None, ALU.subtract).then_inc(s_rnd, 1)
                    nc.vector.tensor_scalar(first[:, :], first[:, :], float(W), float(N), ALU.add, ALU.min).then_inc(s_rnd, 1)
                    hold(dve, carrier["dve"], s_rnd, r * 3 + 3)

        layer0.close()
        yz = [whole.enter_context(nc.sbuf_tensor(f"yz{k}", [B, NB, 2 * D], F16)) for k in range(2)]
        with ExitStack() as scope:
            sb, ps = sb_in(scope), ps_in(scope)
            w1 = sb("w1", [D, D], F32)
            b1c = sb("b1c", [D, 1], F32)
            w2 = sb("w2", [D + 1, D], F32)
            CW = 4 * B
            h1 = [sb(f"h1{k}", [D + 1, CW], F32) for k in range(2)]
            stats = sb("stats", [B, NB, 6], F32)
            mv = sb("mv", [B, NB, 2], F32)
            rs = sb("rs", [B, NB], F32)
            ra = sb("ra", [B, NB], F32)
            rt = sb("rt", [B, NB], F32)
            dg = sb("dg", [B, 2, NB], F32)
            ds_ = sb("ds_", [B, 2, NB], F32)
            dt_ = sb("dt_", [B, 2, NB], F32)
            xs = sb("xs", [B, NB, D], F32)
            ph = [bank(ps, f"ph{k}")[0:D, 0:CW] for k in range(2)]
            po = [bank(ps, f"po{k}")[0:B, :].rearrange("p (j f) -> p j f", j=4) for k in range(2)]
            s_w, s_h, s_hr, s_o, s_oa, s_sq, s_sr, s_v3, s_on = (sem("m_w"), sem("m_h"), sem("m_hr"), sem("m_o"), sem("m_oa"),
                                                               sem("m_sq"), sem("m_sr"), sem("m_v"), sem("m_on"))
            chunks = [(c, min(4, NB - c)) for c in range(0, NB, 4)]
            block = scope.enter_context(nc.Block())

            @block.sync
            def _(sp):
                sp.dma_start(w1[:, :], w1T).then_inc(s_w, 16)
                sp.dma_start(w2[:, :], w2T).then_inc(s_w, 16)
                sp.dma_start(b1c[:, :], b1).then_inc(s_w, 16)
                sp.wait_ge(s_w, 48)

            @block.tensor
            def _(pe):
                pe.wait_ge(s_w, 48)
                pe.wait_ge(s_on, 2)

                def up_product(k):
                    b0, nb = chunks[k]
                    if k >= 2:
                        pe.wait_ge(s_hr, k - 1)
                    nc.tensor.matmul(ph[k % 2][:, 0:nb * B], w1[:, :], acc[0:D, b0 * B:(b0 + nb) * B], start=True, stop=True).then_inc(s_h, 1)

                up_product(0)
                for k, (b0, nb) in enumerate(chunks):
                    if k + 1 < len(chunks):
                        up_product(k + 1)
                    pe.wait_ge(s_hr, k + 1)
                    if k >= 2:
                        pe.wait_ge(s_oa, k - 1)
                    for j in range(nb):
                        nc.tensor.matmul(po[k % 2][:, j, 0:D], h1[k % 2][:, j * B:(j + 1) * B], w2[:, :], start=True, stop=True)
                        last = nc.tensor.matmul(po[k % 2][:, j, D:D + 1], acc[D:D + 1, (b0 + j) * B:(b0 + j + 1) * B],
                                                h1[k % 2][D:D + 1, 0:1], start=True, stop=True)
                    last.then_inc(s_o, 1)

            @block.scalar
            def _(act):
                act.wait_ge(s_w, 48)
                for k, (b0, nb) in enumerate(chunks):
                    act.wait_ge(s_h, k + 1)
                    if k >= 2:
                        act.wait_ge(s_o, k - 1)
                    nc.scalar.activation(h1[k % 2][0:D, 0:nb * B], ph[k % 2][:, 0:nb * B], ACT.Relu, bias=b1c[:, :]).then_inc(s_hr, 1)
                act.wait_ge(s_sq, 1)
                nc.scalar.activation(ra[:, :], rs[:, :], ACT.Sqrt).then_inc(s_sr, 1)
                nc.scalar.activation(ds_[:, :, :], dt_[:, :, :], ACT.Sqrt).then_inc(s_sr, 1)

            @block.vector
            def _(dve):
                made = [0]

                def link(ins):
                    made[0] += 1
                    ins.then_inc(s_v3, 1)
                    dve.wait_ge(s_v3, made[0])

                for k in range(2):
                    nc.vector.memset(h1[k][D:D + 1, :], 1.0).then_inc(s_on, 1)
                for k, (b0, nb) in enumerate(chunks):
                    dve.wait_ge(s_o, k + 1)
                    link(nc.vector.tensor_copy(ideg[:, b0:b0 + nb], po[k % 2][:, 0:nb, D]))
                    xb = X[:, b0:b0 + nb, :]
                    nc.vector.tensor_tensor(xb, xb, po[k % 2][:, 0:nb, 0:D], ALU.add).then_inc(s_oa, 1)
                    dve.wait_ge(s_oa, k + 1)
                    for j in range(nb):
                        last = nc.vector.bn_stats(stats[:, b0 + j, :], X[:, b0 + j, :])
                    link(last)
                    for j in range(nb):
                        last = nc.vector.bn_aggr(mv[:, b0 + j, :], stats[:, b0 + j, :])
                    link(last)
                link(nc.vector.tensor_scalar(rs[:, :], mv[:, :, 1], EPS, None, ALU.add))
                link(nc.vector.tensor_scalar(dg[:, 0, :], odeg[:, :], 1.0, None, ALU.min))
                link(nc.vector.tensor_scalar(dg[:, 1, :], ideg[:, :], 1.0, None, ALU.min))
                link(nc.vector.tensor_scalar(dt_[:, 0, :], odeg[:, :], 1.0, None, ALU.max))
                nc.vector.tensor_scalar(dt_[:, 1, :], ideg[:, :], 1.0, None, ALU.max).then_inc(s_sq, 1)
                dve.wait_ge(s_sr, 2)

                def newton(a, y, t):
                    link(nc.vector.reciprocal(y, y))
                    link(nc.vector.tensor_tensor(t, y, y, ALU.mult))
                    link(nc.vector.tensor_tensor(t, t, a, ALU.mult))
                    link(nc.vector.tensor_scalar(t, t, -0.5, 1.5, ALU.mult, ALU.add))
                    link(nc.vector.tensor_tensor(y, y, t, ALU.mult))

                newton(rs[:, :], ra[:, :], rt[:, :])
                for k in range(2):
                    newton(dt_[:, k, :], ds_[:, k, :], rt[:, :])
                link(nc.vector.scalar_tensor_tensor(out=scl[:, :, :], in0=ds_[:, :, :], scalar=SCALE, in1=dg[:, :, :],
                                                    op0=ALU.mult, op1=ALU.mult))
                full = [B, NB, D]
                link(nc.vector.tensor_tensor(X[:, :, :], X[:, :, :], mv[:, :, 0:1].broadcast_to(full), ALU.subtract))
                link(nc.vector.tensor_tensor(X[:, :, :], X[:, :, :], ra[:, :].unsqueeze(2).broadcast_to(full), ALU.mult))
                for k in range(2):
                    link(nc.vector.tensor_tensor(xs[:, :, :], X[:, :, :], scl[:, k, :].unsqueeze(2).broadcast_to(full), ALU.mult))
                    link(nc.vector.tensor_copy(yz[k][:, :, 0:D], xs[:, :, :]))
                    link(nc.vector.tensor_tensor(yz[k][:, :, D:2 * D], xs[:, :, :], yz[k][:, :, 0:D], ALU.subtract))
                link(nc.vector.memset(acc[:, :], 0.0))

        z, y = yz
        agt = whole.enter_context(nc.sbuf_tensor("agt", [D, N], F32))
        RING = 5
        START = 64
        with ExitStack() as scope:
            sb, ps = sb_in(scope), ps_in(scope)
            T = [sb(f"T{k}", [B, NB, SW], F16) for k in range(2)]
            sel = [sb(f"sel{k}", [P, 500], F32) for k in range(2)]
            goff_i = sb("goff_i", [P, 500], I32)
            goff = sb("goff", [P, 500], F32)
            tk = sb("tk", [P, 500], F32)
            keyt = sb("keyt", [P, NG, 2], F16)
            lot = sb("lot", [P, NG, 2], F16)
            keys = [sb(f"keys{k}", [P, 4 * PAIRS], F16) for k in range(2)]
            los = [sb(f"los{k}", [P, 4 * PAIRS], F16) for k in range(2)]
            yst = [sb(f"yst{k}", [B, 2, 2 * D], F16) for k in range(2)]
            KO = [sb(f"KO{k}", [P, 4, GW], F16) for k in range(RING)]
            LO = [sb(f"LO{k}", [P, 4, B], F16) for k in range(RING)]
            TX = [sb(f"TX{k}", [B, 2, 2, B], F16) for k in range(2)]
            pt = [bank(ps, f"pt{k}")[0:B, 0:2 * GW].rearrange("p (g n) -> p g n", g=2) for k in range(2)]
            px = [bank(ps, f"px{k}", F16)[0:B, 0:4 * P].rearrange("p (b h s) -> p b h s", b=2, h=2) for k in range(2)]
            pg = [bank(ps, f"pg{k}") for k in range(2)]
            pa = bank(ps, "pa")[0:D, 0:SW]
            picked, multiplied, tabled, g_off, g_v = sem("picked"), sem("multiplied"), sem("tabled"), sem("g_off"), sem("g_v")
            staged = sem("staged")
            y_in = sem("y_in")
            hot = sem("hot")
            built = sem("built")
            kept = sem("kept")
            turned = sem("turned")
            held = sem("held")
            summed = sem("summed")
            added = sem("c_added")
            at_done = sem("at_done")
            at_kept = sem("at_kept")
            widths = [(a, min(500, NG - a)) for a in range(0, NG, 500)]
            PICKS = len(widths) * 2 * TC
            RP = STRIPS * PAIRS
            block = scope.enter_context(nc.Block())

            def done(item):
                return item + (START + 1)

            def before(p):
                return {0: 1, 1: 3}.get(p, 2)

            def count(eng):
                return eng.value_load(rounds[0:1, 1:2], min_val=1, max_val=TT)

            def strips(eng, step):
                step(0, None, 0)
                with eng.Fori(0, (STRIPS - 1) // 2) as k:
                    step(eng.snap(k * 2 + 1), eng.snap(k * 2), 1)
                    step(eng.snap(k * 2 + 2), eng.snap(k * 2 + 1), 0)
                step(None, STRIPS - 1, 1)

            @block.gpsimd
            def _(pool):
                nc.gpsimd.iota(goff_i[:, :], pattern=[[GW, 500]], base=0, channel_multiplier=0).then_inc(g_off, 1)
                pool.sem_inc(y_in, START)
                with pool.Fori(0, count(pool)) as r:
                    def step(b, u, k):
                        if b is None:
                            return
                        lag = 1 if isinstance(b, int) else 2
                        hold(pool, carrier["pool"], summed, done(r * RP + (b * PAIRS - lag * PAIRS + PAIRS - 1)))
                        nc.gpsimd.tensor_copy(yst[k][:, :, :], y[:, bass.ds(b * 2, 2), :]).then_inc(y_in, 1)
                    strips(pool, step)

            @block.tensor
            def _(pe):
                for s in (multiplied, built, turned, summed, at_done):
                    pe.sem_inc(s, START)
                with pe.Fori(0, count(pe)) as r:
                    pe.wait_ge(added, done(r * RP - 1))
                    for s in range(PICKS):
                        c, w = s % TC, widths[s // (2 * TC)][1]
                        pe.wait_ge(picked, done(r * PICKS + s))
                        if c == 0:
                            pe.wait_ge(tabled, done(r * (PICKS // TC) + (s // TC - 1)))
                        nc.tensor.matmul(pg[0][:, 0:w], key_te[:, c, :], sel[s % 2][:, 0:w], start=(c == 0), stop=(c == TC - 1))
                        nc.tensor.matmul(pg[1][:, 0:w], lo_te[:, c, :], sel[s % 2][:, 0:w],
                                         start=(c == 0), stop=(c == TC - 1)).then_inc(multiplied, 1)
                    pe.wait_ge(tabled, done(r * (PICKS // TC) + (PICKS // TC - 1)))

                    def step(b, u, k):
                        use = T[1 - k]
                        if b is not None:
                            b_at = pe.snap(r * RP + b * PAIRS)
                        if u is not None:
                            u_at = pe.snap(r * RP + u * PAIRS)
                            pe.wait_ge(kept, done(u_at + (PAIRS - 1)))
                            pe.wait_ge(y_in, done(r * STRIPS + u))
                            pe.wait_ge(at_kept, done(r * STRIPS + u - 1))

                        def sum_slot(p):
                            pe.wait_ge(held, done(u_at + p))
                            pe.wait_ge(added, done(u_at + (p - before(p))))
                            for blk in range(2):
                                for part in range(2):
                                    last = nc.tensor.matmul(pg[p % 2][0:D, 0:SW], yst[1 - k][:, blk, part * D:(part + 1) * D],
                                                            TX[p % 2][:, blk, :, 0:B], start=(blk + part == 0), stop=(blk + part == 2))
                            last.then_inc(summed, 1)

                        for p in range(PAIRS):
                            if b is not None:
                                pe.wait_ge(hot, done(b_at + p))
                                pe.wait_ge(kept, done(b_at + (p - before(p))))
                                for g in range(2):
                                    for j in range(2):
                                        last = nc.tensor.matmul(pt[p % 2][:, g, :], LO[p % RING][:, 2 * g + j, :],
                                                                KO[p % RING][:, 2 * g + j, :], start=(j == 0), stop=(j == 1))
                                last.then_inc(built, 1)
                            if u is not None:
                                pe.wait_ge(held, done(u_at + (p - before(p))))
                                for blk in range(2):
                                    for h in range(2):
                                        last = nc.tensor.transpose(px[p % 2][:, blk, h, 0:B], use[:, 2 * p + h, blk * B:(blk + 1) * B],
                                                                   ident16[0:B, 0:B])
                                last.then_inc(turned, 1)
                                for h in range(2):
                                    for part in range(2):
                                        last = nc.tensor.matmul(pa[:, :], z[:, 2 * p + h, part * D:(part + 1) * D], use[:, 2 * p + h, :],
                                                                start=(p + h + part == 0), stop=(p == PAIRS - 1 and h + part == 2))
                                if p == PAIRS - 1:
                                    last.then_inc(at_done, 1)
                                if p:
                                    sum_slot(p - 1)
                        if u is not None:
                            sum_slot(PAIRS - 1)
                    strips(pe, step)

            @block.scalar
            def _(act):
                act.sem_inc(kept, START)
                act.sem_inc(held, START)
                with act.Fori(0, count(act)) as r:
                    def step(b, u, k):
                        if b is not None:
                            b_at = act.snap(r * RP + b * PAIRS)
                        if u is not None:
                            u_at = act.snap(r * RP + u * PAIRS)
                        for p in range(PAIRS):
                            if b is not None:
                                act.wait_ge(built, done(b_at + p))
                                nc.scalar.activation(T[k][:, :, 2 * G * p:2 * G * (p + 1)].rearrange("s h (g d) -> s g h d", g=2),
                                                     pt[p % 2][:, :, :].rearrange("s g (h d) -> s g h d", h=NB), ACT.Copy).then_inc(kept, 1)
                            if u is not None:
                                act.wait_ge(turned, done(u_at + p))
                                act.wait_ge(summed, done(u_at + (p - before(p))))
                                nc.scalar.activation(TX[p % 2][:, :, :, 0:B], px[p % 2][:, :, :, 0:B], ACT.Copy).then_inc(held, 1)
                    strips(act, step)

            @block.vector
            def _(dve):
                for s in (picked, tabled, hot, added, at_kept):
                    dve.sem_inc(s, START)
                dve.wait_ge(g_off, 1)
                nc.vector.tensor_copy(goff[:, :], goff_i[:, :]).then_inc(g_v, 1)
                nc.vector.memset(agt[:, :], 0.0).then_inc(g_v, 1)
                dve.wait_ge(g_v, 2)
                STEPS = 3 * (PICKS // TC) + 1
                with dve.Fori(0, count(dve)) as r:
                    v = [2]

                    def link(ins):
                        v[0] += 1
                        ins.then_inc(g_v, 1)
                        dve.wait_ge(g_v, r * STEPS + v[0])

                    for s in range(PICKS):
                        c, j, (a, w) = s % TC, s // TC % 2, widths[s // (2 * TC)]
                        dve.wait_ge(multiplied, done(r * PICKS + (s - 2)))
                        nc.vector.tensor_scalar(sel[s % 2][:, 0:w], t0row[:, a:a + w], tneg[:, c:c + 1], -float(j),
                                                ALU.add, ALU.is_equal).then_inc(picked, 1)
                        if c == TC - 1:
                            dve.wait_ge(multiplied, done(r * PICKS + s))
                            link(nc.vector.tensor_tensor(tk[:, 0:w], pg[0][:, 0:w], goff[:, 0:w], ALU.subtract))
                            link(nc.vector.tensor_scalar(tk[:, 0:w], tk[:, 0:w], float(GW * a), 0.0, ALU.subtract, ALU.max))
                            link(nc.vector.tensor_scalar(keyt[:, a:a + w, j], tk[:, 0:w], float(GW + 1), None, ALU.min))
                            nc.vector.tensor_copy(lot[:, a:a + w, j], pg[1][:, 0:w]).then_inc(tabled, 1)
                    hold(dve, carrier["dve"], tabled, done(r * (PICKS // TC) + (PICKS // TC - 1)))

                    def step(b, u, k):
                        if b is not None:
                            b_at = dve.snap(r * RP + b * PAIRS)
                            nc.vector.tensor_copy(keys[k][:, :].rearrange("p (g j) -> p g j", j=2),
                                                  keyt[:, bass.ds(b * (2 * PAIRS), 2 * PAIRS), :]).then_inc(staged, 1)
                            nc.vector.tensor_copy(los[k][:, :].rearrange("p (g j) -> p g j", j=2),
                                                  lot[:, bass.ds(b * (2 * PAIRS), 2 * PAIRS), :]).then_inc(staged, 1)
                            hold(dve, carrier["dve"], staged, r * (2 * STRIPS) + (b * 2 + 2))
                        if u is not None:
                            u_at = dve.snap(r * RP + u * PAIRS)

                        def add_slot(p):
                            dve.wait_ge(summed, done(u_at + p))
                            dve.wait_ge(added, done(u_at + (p - PAIRS)))
                            a = acc[0:D, SW * p:SW * (p + 1)]
                            nc.vector.tensor_tensor(a, a, pg[p % 2][0:D, 0:SW], ALU.add).then_inc(added, 1)

                        for p in range(PAIRS):
                            if b is not None:
                                dve.wait_ge(built, done(b_at + (p - RING)))
                                for m in range(4):
                                    nc.vector.tensor_scalar(KO[p % RING][:, m, :], keytab[:, :], keys[k][:, 4 * p + m:4 * p + m + 1],
                                                            None, ALU.is_equal)
                                nc.vector.tensor_tensor(LO[p % RING][:, :, :], iota16[:, :].unsqueeze(1).broadcast_to([P, 4, B]),
                                                        los[k][:, 4 * p:4 * p + 4].unsqueeze(2).broadcast_to([P, 4, B]),
                                                        ALU.is_equal).then_inc(hot, 1)
                            if u is not None and p >= 2:
                                add_slot(p - 2)
                        if u is not None:
                            add_slot(PAIRS - 2)
                            add_slot(PAIRS - 1)
                            dve.wait_ge(at_done, done(r * STRIPS + u))
                            dve.wait_ge(at_kept, done(r * STRIPS + u - 1))
                            a = agt[:, bass.ds(u * SW, SW)]
                            nc.vector.tensor_tensor(a, a, pa[:, :], ALU.add).then_inc(at_kept, 1)
                    strips(dve, step)
                    nc.vector.tensor_scalar(t0row[:, :], t0row[:, :], 2.0, None, ALU.add).then_inc(g_v, 1)
                    hold(dve, carrier["dve"], g_v, r * STEPS + (2 + STEPS))

        with ExitStack() as scope:
            sb, ps = sb_in(scope), ps_in(scope)
            wsd = sb("wsd", [D, D], F32)
            wds = sb("wds", [D, D], F32)
            bias = [sb(f"bias{k}", [B, D], F32) for k in range(2)]
            coef = sb("coef", [B, 2, NB], F32)
            tmp = [sb(f"tmp{k}", [B, 4, D], F32) for k in range(2)]
            stats = sb("stats5", [B, NB, 6], F32)
            mv = sb("mv5", [B, NB, 2], F32)
            rs = sb("rs5", [B, NB], F32)
            ra = sb("ra5", [B, NB], F32)
            rt = sb("rt5", [B, NB], F32)
            pf = [[bank(ps, f"pf{k}{d}")[0:B, :].rearrange("p (j f) -> p j f", j=4) for d in range(2)] for k in range(2)]
            f_w, f_p, f_a, f_v, f_sq, f_sr, f_x, f_out = (sem("f_w"), sem("f_p"), sem("f_a"), sem("f_v"), sem("f_sq"), sem("f_sr"),
                                                         sem("f_x"), sem("f_out"))
            block = scope.enter_context(nc.Block())

            @block.sync
            def _(sp):
                sp.dma_start(wsd[:, :], wsdT).then_inc(f_w, 16)
                sp.dma_start(wds[:, :], wdsT).then_inc(f_w, 16)
                sp.dma_start(bias[0][:, :], bsd.broadcast_to([B, D])).then_inc(f_w, 16)
                sp.dma_start(bias[1][:, :], bds.broadcast_to([B, D])).then_inc(f_w, 16)
                ob = out.rearrange("(b p) f -> p b f", p=B)
                sp.wait_ge(f_x, 1)
                sp.dma_start(ob[0:112, :, :], X[0:112, :, :]).then_inc(f_out, 16)
                sp.dma_start(ob[112:B, :, :], X[112:B, :, :]).then_inc(f_out, 16)
                sp.wait_ge(f_out, 32)

            @block.tensor
            def _(pe):
                pe.wait_ge(f_w, 64)
                for k, (b0, nb) in enumerate(chunks):
                    if k >= 2:
                        pe.wait_ge(f_a, k - 1)
                    for d, (src, w) in enumerate(((acc, wsd), (agt, wds))):
                        for j in range(nb):
                            last = nc.tensor.matmul(pf[k % 2][d][:, j, 0:D], src[0:D, (b0 + j) * B:(b0 + j + 1) * B], w[:, :],
                                                    start=True, stop=True)
                    last.then_inc(f_p, 1)

            @block.scalar
            def _(act):
                act.wait_ge(f_sq, 1)
                nc.scalar.activation(ra[:, :], rs[:, :], ACT.Sqrt).then_inc(f_sr, 1)

            @block.vector
            def _(dve):
                made = [0]

                def link(ins):
                    made[0] += 1
                    ins.then_inc(f_v, 1)
                    dve.wait_ge(f_v, made[0])

                link(nc.vector.tensor_scalar(coef[:, :, :], scl[:, :, :], 0.5 / SCALE / SCALE, None, ALU.mult))
                dve.wait_ge(f_w, 64)
                link(nc.vector.tensor_tensor(bias[0][:, :], bias[0][:, :], bias[1][:, :], ALU.add))
                link(nc.vector.tensor_scalar(bias[0][:, :], bias[0][:, :], 0.5, None, ALU.mult))
                full = [B, NB, D]
                link(nc.vector.tensor_tensor(X[:, :, :], X[:, :, :], bias[0][:, :].unsqueeze(1).broadcast_to(full), ALU.add))
                for k, (b0, nb) in enumerate(chunks):
                    dve.wait_ge(f_p, k + 1)
                    xb = X[:, b0:b0 + nb, :]
                    for d in range(2):
                        last = nc.vector.tensor_tensor(tmp[d][:, 0:nb, :], pf[k % 2][d][:, 0:nb, 0:D],
                                                       coef[:, d, b0:b0 + nb].unsqueeze(2).broadcast_to([B, nb, D]), ALU.mult)
                    last.then_inc(f_a, 1)
                    dve.wait_ge(f_a, k + 1)
                    for d in range(2):
                        link(nc.vector.tensor_tensor(xb, xb, tmp[d][:, 0:nb, :], ALU.add))
                    for j in range(nb):
                        last = nc.vector.bn_stats(stats[:, b0 + j, :], X[:, b0 + j, :])
                    link(last)
                    for j in range(nb):
                        last = nc.vector.bn_aggr(mv[:, b0 + j, :], stats[:, b0 + j, :])
                    link(last)
                nc.vector.tensor_scalar(rs[:, :], mv[:, :, 1], EPS, None, ALU.add).then_inc(f_sq, 1)
                dve.wait_ge(f_sr, 1)
                link(nc.vector.reciprocal(ra[:, :], ra[:, :]))
                link(nc.vector.tensor_tensor(rt[:, :], ra[:, :], ra[:, :], ALU.mult))
                link(nc.vector.tensor_tensor(rt[:, :], rt[:, :], rs[:, :], ALU.mult))
                link(nc.vector.tensor_scalar(rt[:, :], rt[:, :], -0.5, 1.5, ALU.mult, ALU.add))
                link(nc.vector.tensor_tensor(ra[:, :], ra[:, :], rt[:, :], ALU.mult))
                link(nc.vector.tensor_tensor(X[:, :, :], X[:, :, :], mv[:, :, 0:1].broadcast_to(full), ALU.subtract))
                nc.vector.tensor_tensor(X[:, :, :], X[:, :, :], ra[:, :].unsqueeze(2).broadcast_to(full), ALU.mult).then_inc(f_x, 1)


def kernel(x, src, dst, edge_attr_96, L0_gnn_W_edge, L0_gnn_b_edge, L0_gnn_eps, L0_gnn_W1, L0_gnn_b1, L0_gnn_W2, L0_gnn_b2,
           L1_gnn_W_sd, L1_gnn_b_sd, L1_gnn_W_ds, L1_gnn_b_ds):
    import numpy as np
    import concourse.bacc as bacc
    from concourse.bass_utils import run_bass_kernel_spmd

    def padded(a, fill, n):
        out = np.full((n,), fill, np.int32)
        out[:E] = np.asarray(a)
        return out

    def by_tile(a):
        return np.ascontiguousarray(padded(a, N, TT * P).reshape(TC, P, P).transpose(1, 0, 2).reshape(P, TT))

    def by_edge(a):
        return np.ascontiguousarray(padded(a, N, TILES * P).reshape(TILES, P).T)

    def with_bias(w, b):
        return np.ascontiguousarray(np.concatenate([np.asarray(w).T, np.asarray(b)[None, :]], axis=0))

    x = np.ascontiguousarray(x)
    ea = np.zeros((D, TILES * P), np.float32)
    ea[:, :E] = np.asarray(edge_attr_96).T
    arrays = {
        "x": x,
        "xT": np.ascontiguousarray(x.T),
        "dst_te": by_tile(dst), "src_te": by_tile(src),
        "dst_et": by_edge(dst), "src_et": by_edge(src),
        "src_gather": np.ascontiguousarray(padded(src, 0, TILES * P).reshape(2 * CH, HT, P).transpose(0, 2, 1)),
        "eaT": ea,
        "weT": with_bias(L0_gnn_W_edge, L0_gnn_b_edge),
        "w1T": np.ascontiguousarray(np.asarray(L0_gnn_W1).T),
        "b1": np.ascontiguousarray(L0_gnn_b1).reshape(D, 1),
        "w2T": with_bias(L0_gnn_W2, L0_gnn_b2),
        "eps": np.ascontiguousarray(L0_gnn_eps).reshape(1, 1),
        "wsdT": np.ascontiguousarray(np.asarray(L1_gnn_W_sd).T),
        "wdsT": np.ascontiguousarray(np.asarray(L1_gnn_W_ds).T),
        "bsd": np.ascontiguousarray(L1_gnn_b_sd).reshape(1, D),
        "bds": np.ascontiguousarray(L1_gnn_b_ds).reshape(1, D),
    }
    nc = bacc.Bacc("TRN2", target_bir_lowering=False, num_devices=1)
    args = [nc.dram_tensor("in_" + k, a.shape, mybir.dt.from_np(a.dtype), kind="ExternalInput").ap() for k, a in arrays.items()]
    out = nc.dram_tensor("out", (N, D), F32, kind="ExternalOutput").ap()
    gnn(nc, *args, out)
    result = run_bass_kernel_spmd(nc, [{"in_" + k: a for k, a in arrays.items()}], core_ids=[0])
    return result.results[0]["out"]
```

```python
from contextlib import ExitStack

import concourse.bass as bass
from concourse import mybir

F32, F16, I32 = mybir.dt.float32, mybir.dt.float16, mybir.dt.int32
ALU, ACT, AX = mybir.AluOpType, mybir.ActivationFunctionType, mybir.AxisListType

N, E, D = 6250, 100000, 96
P = 128
B = 125
NB = N // B
HT = 8
CH = -(-E // (2 * HT * P))
TILES = 2 * HT * CH
TC = -(-TILES // P)
TT = TC * P
W = 32
ACCW = N + W + 6
G = 5
NG = N // G
GC = -(-NG // P)
GW = G * NB
PAIRS = 25
STRIPS = NG // (2 * PAIRS)
SW = 2 * B
SCALE = 1024.0
EPS = 1e-5


def bank(ps, name, dt=F32):
    return ps(name, [P, 512 if dt == F32 else 1024], dt)


def hold(eng, carrier, sem, value):
    eng.wait_ge(sem, value)
    eng.sem_inc(carrier, 1)


def norm_buffers(sb, tag):
    return [sb(f"{tag}_{n}", [B, NB, w], F32) for n, w in (("stats", 6), ("mv", 2), ("var", 1), ("inv", 1), ("off", 1), ("tmp", 1))]


def statistics(nc, dve, link, norm, X, k, b0, nb, s_sq):
    stats, mv, var = norm[:3]
    for b in range(b0, b0 + nb):
        last = nc.vector.bn_stats(stats[:, b, :], X[:, b, :])
    link(last)
    for b in range(b0, b0 + nb):
        last = nc.vector.bn_aggr(mv[:, b, :], stats[:, b, :])
    link(last)
    nc.vector.tensor_scalar(var[:, b0:b0 + nb, 0], mv[:, b0:b0 + nb, 1], EPS, None, ALU.add).then_inc(s_sq, 1)


def inverse_root(nc, dve, link, norm, k, b0, nb, s_sr, s_nm):
    _, mv, var, inv, off, tmp = norm
    v, i, o, t = (a[:, b0:b0 + nb, 0] for a in (var, inv, off, tmp))
    dve.wait_ge(s_sr, k + 1)
    link(nc.vector.reciprocal(i, i))
    link(nc.vector.tensor_tensor(t, i, i, ALU.mult))
    link(nc.vector.tensor_tensor(t, t, v, ALU.mult))
    link(nc.vector.tensor_scalar(t, t, -0.5, 1.5, ALU.mult, ALU.add))
    link(nc.vector.tensor_tensor(i, i, t, ALU.mult))
    nc.vector.scalar_tensor_tensor(out=o, in0=mv[:, b0:b0 + nb, 0], scalar=-1.0, in1=i, op0=ALU.mult, op1=ALU.mult).then_inc(s_nm, 1)


def apply_norm(nc, act, norm, X, k, b0, nb, s_sq, s_sr, s_nm, s_ap):
    _, _, var, inv, off, _ = norm
    act.wait_ge(s_sq, k + 1)
    nc.scalar.activation(inv[:, b0:b0 + nb, 0], var[:, b0:b0 + nb, 0], ACT.Sqrt).then_inc(s_sr, 1)
    act.wait_ge(s_nm, k + 1)
    for b in range(b0, b0 + nb):
        last = nc.scalar.activation(X[:, b, :], X[:, b, :], ACT.Identity, bias=off[:, b, :], scale=inv[:, b, :])
    last.then_inc(s_ap, 1)


def gnn(nc, x, xT, dst_te, src_te, dst_et, src_et, src_gather, eaT, weT, w1T, b1, w2T, eps, wsdT, wdsT, bsd, bds, out):
    nc.disable_value_cache = True
    whole = ExitStack()

    def sb_in(scope):
        return lambda name, shape, dt: scope.enter_context(nc.sbuf_tensor(name, shape, dt))

    def ps_in(scope):
        return lambda name, shape, dt: scope.enter_context(nc.psum_tensor(name, shape, dt))

    def sem(name):
        return whole.enter_context(nc.semaphore(name))

    with whole:
        sb = sb_in(whole)
        carrier = {e: sem(f"carrier_{e}") for e in ("pool", "dve")}
        acc = sb("acc", [D + 1, ACCW], F32)
        X = sb("X", [B, NB, D], F32)
        lo_te = sb("lo_te", [P, TC, P], F16)
        da_te = sb("da_te", [P, TC, P], F16)
        db_te = sb("db_te", [P, TC, P], F16)
        rounds = sb("rounds", [1, 2], I32)
        t0row = sb("t0row", [P, GC * P], F16)
        tneg = sb("tneg", [P, TC], F32)
        iota16 = sb("iota16", [P, B], F16)
        keytab = sb("keytab", [P, GW], F16)
        ident = sb("ident", [P, P], F32)
        ident16 = sb("ident16", [P, P], F16)
        odeg = sb("odeg", [B, NB], F32)
        ideg = sb("ideg", [B, NB], F32)
        scl = sb("scl", [B, 2, NB], F32)
        bias = [sb(f"bias{k}", [B, D], F32) for k in range(2)]

        layer0 = ExitStack()
        sb = sb_in(layer0)
        dloc = sb("dloc", [P, TILES], F32)
        hi_et = sb("hi_et", [P, TILES], F16)
        lo_et = sb("lo_et", [P, TILES], F16)
        iotaw = sb("iotaw", [P, W], F32)
        first = sb("first", [1, TILES], I32)
        di = sb("di", [P, TT], I32)
        si = sb("si", [P, TT], I32)
        qi = sb("qi", [P, TT], I32)
        ones = sb("ones", [P, P], F32)
        wide = sb("wide", [P, 4, P], F32)
        cols = sb("cols", [P, 2 * TC + 2 * GC], F32)
        row = sb("row", [P, 2 * TC + 2 * GC, P], F32)
        up_i = sb("up_i", [P, TT], I32)
        up = sb("up", [P, TT], F32)
        down = sb("down", [P, TT], F32)
        reach = [sb(f"reach{k}", [P, TT], F32) for k in range(2)]
        thr_i = sb("thr_i", [P, GC], I32)
        thr = sb("thr", [P, 2, GC], F32)
        mask = sb("mask", [P, GC], F32)
        ends = sb("ends", [P, 2, GC], F32)
        rnf = sb("rnf", [1, 2], F32)
        rni = sb("rni", [1, 2], I32)
        tmin = row[:, 0:TC, :].rearrange("p c t -> p (c t)")
        tmax = row[:, TC:2 * TC, :].rearrange("p c t -> p (c t)")

        def high(dve, link, s, q):
            link(nc.vector.tensor_scalar(q, s, 8389.0, None, ALU.mult))
            link(nc.vector.tensor_scalar(q, q, 20, None, ALU.arith_shift_right))

        def rows(dve, link, k0, k1, s_wide, s_row, pr):
            for k in range(k0, k1):
                if k - k0 >= 4:
                    dve.wait_ge(s_row, k - k0 - 3)
                nc.vector.tensor_scalar(wide[:, k % 4, :], ones[:, :], cols[:, k:k + 1], None, ALU.mult).then_inc(s_wide, 1)
            for n, k in enumerate(range(k0, k1, 4)):
                m = min(4, k1 - k)
                dve.wait_ge(s_row, k - k0 + m)
                link(nc.vector.tensor_copy(row[:, k:k + m, :], pr[n][:, 0:m, :]))

        def row_products(pe, k0, k1, s_wide, s_row, pr):
            for k in range(k0, k1):
                pe.wait_ge(s_wide, k - k0 + 1)
                nc.tensor.matmul(pr[(k - k0) // 4][:, (k - k0) % 4, :], wide[:, k % 4, :], ident[:, :],
                                 start=True, stop=True).then_inc(s_row, 1)

        with ExitStack() as scope:
            sb, ps = sb_in(scope), ps_in(scope)
            dei = sb("dei", [P, TILES], I32)
            sei = sb("sei", [P, TILES], I32)
            tneg_i = sb("tneg_i", [P, TC], I32)
            key_i = sb("key_i", [P, GW], I32)
            epsc = sb("epsc", [D, 1], F32)
            eps1 = sb("eps1", [D, 1], F32)
            pr = [ps(f"pr{i}", [P, 4, P], F32) for i in range(4)]
            s_di, s_si, s_dei, s_sei, s_x, s_eps, s_b = (sem("s_di"), sem("s_si"), sem("s_dei"), sem("s_sei"), sem("s_x"),
                                                         sem("s_eps"), sem("s_b"))
            s_const, s_id, s_wide, s_row, s_v, s_e1, s_acc = (sem("s_const"), sem("s_id"), sem("s_wide"), sem("s_row"),
                                                              sem("s_v"), sem("s_e1"), sem("s_acc"))
            block = scope.enter_context(nc.Block())

            @block.sync
            def _(sp):
                sp.dma_start(di[:, :], dst_te).then_inc(s_di, 16)
                sp.dma_start(sei[:, :], src_et).then_inc(s_sei, 16)
                sp.dma_start(dei[:, :], dst_et).then_inc(s_dei, 16)
                sp.dma_start(epsc[:, :], eps.broadcast_to([D, 1])).then_inc(s_eps, 16)
                sp.dma_start(acc[0:D, 0:N], xT).then_inc(s_x, 16)
                sp.dma_start(si[:, :], src_te).then_inc(s_si, 16)
                sp.dma_start(bias[0][:, :], bsd.broadcast_to([B, D])).then_inc(s_b, 16)
                sp.dma_start(bias[1][:, :], bds.broadcast_to([B, D])).then_inc(s_b, 16)
                sp.wait_ge(s_si, 16)
                sp.wait_ge(s_b, 32)

            @block.gpsimd
            def _(pool):
                nc.gpsimd.memset(ident[:, :], 0.0).then_inc(s_id, 1)
                nc.gpsimd.memset(ident16[:, :], 0.0).then_inc(s_id, 1)
                nc.gpsimd.memset(ones[:, :], 1.0).then_inc(s_const, 1)
                pool.wait_ge(s_id, 2)
                for m in (ident, ident16):
                    nc.gpsimd.affine_select(out=m[:, :], in_=m[:, :], compare_op=ALU.not_equal, fill=1.0, base=0,
                                            pattern=[[-1, P]], channel_multiplier=1).then_inc(s_id, 1)
                nc.gpsimd.iota(up_i[:, :], pattern=[[1, TT]], base=0, channel_multiplier=0).then_inc(s_const, 1)
                nc.gpsimd.iota(thr_i[:, :], pattern=[[G * P, GC]], base=0, channel_multiplier=G).then_inc(s_const, 1)
                nc.gpsimd.iota(tneg_i[:, :], pattern=[[-P, TC]], base=0, channel_multiplier=-1).then_inc(s_const, 1)
                nc.gpsimd.iota(key_i[:, :], pattern=[[1, NB], [NB, G]], base=1, channel_multiplier=0).then_inc(s_const, 1)

            @block.tensor
            def _(pe):
                pe.wait_ge(s_id, 4)
                row_products(pe, 0, 2 * TC, s_wide, s_row, pr)

            @block.scalar
            def _(act):
                act.wait_ge(s_eps, 16)
                nc.scalar.activation(eps1[:, :], epsc[:, :], ACT.Copy, bias=1.0).then_inc(s_e1, 1)
                act.wait_ge(s_e1, 1)
                act.wait_ge(s_x, 16)
                nc.scalar.activation(acc[0:D, 0:N], acc[0:D, 0:N], ACT.Copy, scale=eps1[:, :]).then_inc(s_acc, 1)

            @block.vector
            def _(dve):
                made = [0]

                def link(ins):
                    made[0] += 1
                    ins.then_inc(s_v, 1)
                    dve.wait_ge(s_v, made[0])

                nc.vector.memset(acc[0:D, N:ACCW], 0.0)
                nc.vector.memset(acc[D:D + 1, :], 0.0)
                dve.wait_ge(s_di, 16)
                for k, op in enumerate((ALU.min, ALU.max)):
                    link(nc.vector.tensor_reduce(cols[:, k * TC:(k + 1) * TC], di[:, :].rearrange("p (c e) -> p c e", c=TC), AX.X, op))
                dve.wait_ge(s_const, 1)
                rows(dve, link, 0, 2 * TC, s_wide, s_row, pr)
                dve.wait_ge(s_sei, 16)
                q = qi[:, 0:TILES]
                high(dve, link, sei[:, :], q)
                nc.vector.tensor_copy(hi_et[:, :], q)
                nc.vector.scalar_tensor_tensor(out=lo_et[:, :], in0=q, scalar=-float(B), in1=sei[:, :], op0=ALU.mult, op1=ALU.add)
                dve.wait_ge(s_dei, 16)
                nc.vector.tensor_tensor(dloc[:, :], dei[:, :], tmin[:, 0:TILES], ALU.subtract)
                nc.vector.tensor_copy(first[:, :], tmin[0:1, 0:TILES])
                dve.wait_ge(s_const, 5)
                nc.vector.tensor_copy(iota16[:, :], up_i[:, 0:B])
                nc.vector.tensor_copy(iotaw[:, :], up_i[:, 0:W])
                nc.vector.tensor_copy(keytab[:, :], key_i[:, :])
                nc.vector.tensor_copy(tneg[:, :], tneg_i[:, :])
                nc.vector.tensor_copy(thr[:, 0, :], thr_i[:, :])
                nc.vector.tensor_scalar(thr[:, 1, :], thr_i[:, :], float(G - 1), None, ALU.add)
                nc.vector.tensor_scalar(mask[:, :], thr_i[:, :], float(N), None, ALU.is_lt)
                nc.vector.tensor_scalar(down[:, :], up_i[:, :], -1.0, float(TT), ALU.mult, ALU.add)
                nc.vector.tensor_scalar(up[:, :], up_i[:, :], 1.0, None, ALU.add)
                link(nc.vector.tensor_tensor(reach[0][0:1, :], tmax[0:1, :], tmin[0:1, :], ALU.subtract))
                link(nc.vector.tensor_reduce(rnf[:, 0:1], reach[0][0:1, :], AX.X, ALU.max))
                link(nc.vector.tensor_scalar(rni[:, 0:1], rnf[:, 0:1], float(W), None, ALU.add))
                link(nc.vector.tensor_scalar(rounds[:, 0:1], rni[:, 0:1], W.bit_length() - 1, None, ALU.arith_shift_right))

        with ExitStack() as scope:
            sb, ps = sb_in(scope), ps_in(scope)
            we = sb("we", [D + 1, D], F32)
            ea = [sb(f"ea{h}", [D + 1, HT * P], F32) for h in range(2)]
            idx = [sb(f"idx{h}", [P, HT], I32) for h in range(2)]
            msg = [sb(f"msg{k}", [P, 4, D + 1], F32) for k in range(4)]
            win = [sb(f"win{q}", [P, 4, W], F32) for q in range(2)]
            lo1 = [sb(f"lo1{q}", [P, 4, B], F16) for q in range(2)]
            hi1 = [sb(f"hi1{q}", [P, 4, NB], F16) for q in range(2)]
            pm = [bank(ps, f"pm{q}")[:, 0:4 * D].rearrange("p (j f) -> p j f", j=4) for q in range(2)]
            pw = [bank(ps, f"pw{q}")[0:D + 1, 0:4 * W].rearrange("p (j w) -> p j w", j=4) for q in range(2)]
            pd = [bank(ps, f"pd{h}")[0:B, 0:NB] for h in range(2)]
            s_we, s_one, s_x2 = sem("s_we"), sem("s_one"), sem("s_x2")
            ea_in = [sem(f"ea_in{h}") for h in range(2)]
            idx_in = [sem(f"idx_in{h}") for h in range(2)]
            xg_in = [sem(f"xg_in{k}") for k in range(4)]
            CREDIT = 2
            prod_done = [sem(f"prod_done{q}") for q in range(2)]
            sum_done = [sem(f"sum_done{q}") for q in range(2)]
            relu_done = [sem(f"relu_done{q}") for q in range(2)]
            hot_done = [sem(f"hot_done{q}") for q in range(2)]
            seg_done = [sem(f"seg_done{q}") for q in range(2)]
            added, s_rnd, s_te, s_end = sem("added"), sem("s_rnd"), sem("s_te"), sem("s_end")
            block = scope.enter_context(nc.Block())

            def count(eng):
                return eng.value_load(rounds[0:1, 0:1], min_val=1, max_val=N)

            def quarter(n, h):
                return n * 2 + (h + 1 + CREDIT)

            @block.sync
            def _(sp):
                sp.dma_start(we[:, :], weT).then_inc(s_we, 16)
                xb = x.rearrange("(b p) f -> p b f", p=B)
                sp.dma_start(X[0:112, :, :], xb[0:112, :, :]).then_inc(s_x2, 16)
                sp.dma_start(X[112:B, :, :], xb[112:B, :, :]).then_inc(s_x2, 16)
                sp.wait_ge(s_one, 2)
                with sp.Fori(0, count(sp)) as r:
                    with sp.Fori(0, CH) as i:
                        n = sp.snap(r * CH + i)
                        for h in range(2):
                            sp.wait_ge(sum_done[1], quarter(n - 1, h))
                            sp.dma_start(idx[h][:, :], src_gather[bass.ds(i * 2 + h, 1), :, :].rearrange("a p t -> (a p) t")).then_inc(idx_in[h], 16)
                            sp.wait_ge(prod_done[1], quarter(n - 1, h))
                            sp.dma_start(ea[h][0:D, :], eaT[:, bass.ds(i * (2 * HT * P) + h * HT * P, HT * P)]).then_inc(ea_in[h], 16)
                sp.wait_ge(s_x2, 32)

            @block.gpsimd
            def _(pool):
                with pool.Fori(0, count(pool)) as r:
                    with pool.Fori(0, CH) as i:
                        n = pool.snap(r * CH + i)
                        for h in range(2):
                            hold(pool, carrier["pool"], idx_in[h], n * 16 + 16)
                            for q in range(2):
                                hold(pool, carrier["pool"], seg_done[q], quarter(n - 1, h))
                                for j in range(4):
                                    nc.gpsimd.indirect_dma_start(out=msg[2 * h + q][:, j, 0:D], out_offset=None, in_=x[:, :],
                                                                 in_offset=bass.IndirectOffsetOnAxis(ap=idx[h][:, 4 * q + j:4 * q + j + 1], axis=0)
                                                                 ).then_inc(xg_in[2 * h + q], 16)

            @block.tensor
            def _(pe):
                for s in prod_done + seg_done:
                    pe.sem_inc(s, CREDIT)
                pe.wait_ge(s_we, 16)
                with pe.Fori(0, count(pe)) as r:
                    with pe.Fori(0, CH) as i:
                        n = pe.snap(r * CH + i)

                        def products(k):
                            h, q = divmod(k, 2)
                            if q == 0:
                                pe.wait_ge(ea_in[h], n * 16 + 16)
                            for j in range(4):
                                t = 4 * q + j
                                last = nc.tensor.matmul(pm[q][:, j, :], ea[h][:, t * P:(t + 1) * P], we[:, :], start=True, stop=True)
                            last.then_inc(prod_done[q], 1)

                        def segments(k):
                            h, q = divmod(k, 2)
                            pe.wait_ge(relu_done[q], quarter(n, h))
                            pe.wait_ge(hot_done[q], quarter(n, h))
                            for j in range(4):
                                nc.tensor.matmul(pw[q][:, j, :], msg[k][:, j, :], win[q][:, j, :], start=True, stop=True)
                            for j in range(4):
                                last = nc.tensor.matmul(pd[h][:, :], lo1[q][:, j, :], hi1[q][:, j, :],
                                                        start=(q == 0 and j == 0), stop=(q == 1 and j == 3))
                            last.then_inc(seg_done[q], 1)

                        products(0)
                        for k in range(1, 4):
                            products(k)
                            segments(k - 1)
                        segments(3)

            @block.scalar
            def _(act):
                for s in relu_done:
                    act.sem_inc(s, CREDIT)
                with act.Fori(0, count(act)) as r:
                    with act.Fori(0, CH) as i:
                        n = act.snap(r * CH + i)
                        for k in range(4):
                            act.wait_ge(sum_done[k % 2], quarter(n, k // 2))
                            nc.scalar.activation(msg[k][:, :, 0:D], msg[k][:, :, 0:D], ACT.Relu).then_inc(relu_done[k % 2], 1)

            @block.vector
            def _(dve):
                for s in sum_done + hot_done:
                    dve.sem_inc(s, CREDIT)
                for h in range(2):
                    nc.vector.memset(ea[h][D:D + 1, :], 1.0).then_inc(s_one, 1)
                for k in range(4):
                    nc.vector.memset(msg[k][:, :, D:D + 1], 1.0)
                regs = [dve.alloc_register(f"first_node{k}") for k in range(2 * HT)]

                def steps(r, i):
                    n = dve.snap(r * CH + i)
                    dve.load(regs, first[0:1, bass.ds(i * (2 * HT), 2 * HT)])
                    node = [dve.snap(g, min_val=0, max_val=N) for g in regs]

                    def onehots(k):
                        t0, q = i * (2 * HT) + 4 * k, k % 2
                        for table, ruler, hot, w in ((dloc, iotaw, win, W), (lo_et, iota16, lo1, B), (hi_et, iota16, hi1, NB)):
                            last = nc.vector.tensor_tensor(
                                hot[q][:, :, :], ruler[:, 0:w].unsqueeze(1).broadcast_to([P, 4, w]),
                                table[:, bass.ds(t0, 4)].unsqueeze(2).broadcast_to([P, 4, w]), ALU.is_equal)
                        last.then_inc(hot_done[q], 1)

                    def add_source(k):
                        dve.wait_ge(prod_done[k % 2], quarter(n, k // 2))
                        dve.wait_ge(xg_in[k], n * 64 + 64)
                        nc.vector.tensor_tensor(msg[k][:, :, 0:D], msg[k][:, :, 0:D], pm[k % 2][:, :, :], ALU.add).then_inc(sum_done[k % 2], 1)

                    def accumulate(k):
                        h, q = divmod(k, 2)
                        dve.wait_ge(seg_done[q], quarter(n, h))
                        for j in range(4):
                            a = acc[:, bass.ds(node[4 * k + j], W)]
                            nc.vector.tensor_tensor(a, a, pw[q][:, j, :], ALU.add).then_inc(added, 1)
                            hold(dve, carrier["dve"], added, n * 18 + (4 * k + j + 1 + h))
                        if q:
                            nc.vector.tensor_tensor(odeg[:, :], odeg[:, :], pd[h][:, :], ALU.add).then_inc(added, 1)
                            hold(dve, carrier["dve"], added, n * 18 + 9 * (h + 1))

                    onehots(0)
                    add_source(0)
                    for k in range(1, 4):
                        onehots(k)
                        add_source(k)
                        accumulate(k - 1)
                    accumulate(3)

                with dve.Fori(0, count(dve)) as r:
                    EV = 3 + 4 * GC + 8
                    nc.vector.memset(odeg[:, :], 0.0).then_inc(s_rnd, 1)
                    hold(dve, carrier["dve"], s_rnd, r * EV + 1)
                    with dve.Fori(0, GC) as c:
                        steps(r, c)
                        v = r * EV + c * 4
                        for e, (tiles, op, ruler) in enumerate(((tmax, ALU.is_ge, down), (tmin, ALU.is_le, up))):
                            nc.vector.scalar_tensor_tensor(out=reach[e][:, :], in0=tiles, scalar=thr[:, e, bass.ds(c, 1)], in1=ruler[:, :],
                                                           op0=op, op1=ALU.mult).then_inc(s_rnd, 1)
                            dve.wait_ge(s_rnd, v + (2 * e + 2))
                            nc.vector.tensor_reduce(ends[:, e, bass.ds(c, 1)], reach[e][:, :], AX.X, ALU.max).then_inc(s_rnd, 1)
                        hold(dve, carrier["dve"], s_rnd, v + 5)
                    done = [4 * GC + 1]

                    def link(ins):
                        done[0] += 1
                        ins.then_inc(s_rnd, 1)
                        dve.wait_ge(s_rnd, r * EV + done[0])

                    flat = "p c e -> p (c e)"
                    high(dve, link, si[:, :], qi[:, :])
                    link(nc.vector.scalar_tensor_tensor(out=lo_te[:, :, :].rearrange(flat), in0=qi[:, :], scalar=-float(B), in1=si[:, :],
                                                        op0=ALU.mult, op1=ALU.add))
                    ri = reach[0][:, :].bitcast(I32)
                    link(nc.vector.tensor_scalar(ri, di[:, :], 3, None, ALU.arith_shift_right))
                    link(nc.vector.tensor_copy(da_te[:, :, :].rearrange(flat), ri))
                    link(nc.vector.scalar_tensor_tensor(out=reach[1][:, :], in0=ri, scalar=-8.0, in1=di[:, :], op0=ALU.mult, op1=ALU.add))
                    link(nc.vector.tensor_scalar(qi[:, :], qi[:, :], 1.0, None, ALU.add))
                    link(nc.vector.scalar_tensor_tensor(out=db_te[:, :, :].rearrange(flat), in0=reach[1][:, :], scalar=float(NB), in1=qi[:, :],
                                                        op0=ALU.mult, op1=ALU.add))
                    hold(dve, carrier["dve"], s_rnd, r * EV + done[0])
                    with dve.Fori(GC, CH) as i:
                        steps(r, i)
                    link(nc.vector.tensor_scalar(dloc[:, :], dloc[:, :], float(W), None, ALU.subtract))
                    nc.vector.tensor_scalar(first[:, :], first[:, :], float(W), float(N), ALU.add, ALU.min).then_inc(s_rnd, 1)
                    done[0] += 1
                    hold(dve, carrier["dve"], s_rnd, r * EV + done[0])
                    assert done[0] == EV, (done, EV)

        with ExitStack() as scope:
            ps = ps_in(scope)
            pr = [ps(f"qr{i}", [P, 4, P], F32) for i in range(5)]
            pdeg = bank(ps, "pdeg")
            t_wide, t_row, t_v, t_b, t_deg, t_sq = sem("t_wide"), sem("t_row"), sem("t_v"), sem("t_b"), sem("t_deg"), sem("t_sq")
            dg = layer0.enter_context(nc.sbuf_tensor("dg", [B, 2, NB], F32))
            dmax = layer0.enter_context(nc.sbuf_tensor("dmax", [B, 2, NB], F32))
            droot = layer0.enter_context(nc.sbuf_tensor("droot", [B, 2, NB], F32))
            dtmp = layer0.enter_context(nc.sbuf_tensor("dtmp", [B, 2, NB], F32))
            block = scope.enter_context(nc.Block())

            @block.tensor
            def _(pe):
                for b in range(NB):
                    last = nc.tensor.matmul(pdeg[0:B, b:b + 1], acc[D:D + 1, b * B:(b + 1) * B], ident[D:D + 1, D:D + 1],
                                            start=True, stop=True)
                last.then_inc(t_deg, 1)
                row_products(pe, 2 * TC, 2 * TC + 2 * GC, t_wide, t_row, pr)

            @block.scalar
            def _(act):
                act.wait_ge(t_sq, 1)
                nc.scalar.activation(droot[:, :, :], dmax[:, :, :], ACT.Sqrt).then_inc(t_sq, 1)

            @block.vector
            def _(dve):
                made = [0]

                def link(ins):
                    made[0] += 1
                    ins.then_inc(t_v, 1)
                    dve.wait_ge(t_v, made[0])

                k0 = 2 * TC
                link(nc.vector.tensor_scalar(cols[:, k0:k0 + GC], ends[:, 0, :], -1.0, float(TT), ALU.mult, ALU.add))
                link(nc.vector.tensor_tensor(ends[:, 1, :], ends[:, 1, :], ends[:, 0, :], ALU.add))
                link(nc.vector.tensor_scalar(ends[:, 1, :], ends[:, 1, :], float(TT), None, ALU.subtract))
                link(nc.vector.tensor_tensor(cols[:, k0 + GC:], ends[:, 1, :], mask[:, :], ALU.mult))
                rows(dve, link, k0, k0 + 2 * GC, t_wide, t_row, pr)
                link(nc.vector.tensor_copy(t0row[:, :], row[:, k0:k0 + GC, :].rearrange("p c t -> p (c t)")))
                link(nc.vector.tensor_reduce(rnf[:, 1:2], row[0:1, k0 + GC:, :], AX.XY, ALU.max))
                link(nc.vector.tensor_scalar(rni[:, 1:2], rnf[:, 1:2], 1.0, 2.0, ALU.add, ALU.max))
                link(nc.vector.tensor_scalar(rounds[:, 1:2], rni[:, 1:2], 1, None, ALU.arith_shift_right))
                dve.wait_ge(t_deg, 1)
                link(nc.vector.tensor_copy(ideg[:, :], pdeg[0:B, 0:NB]))
                for k, deg in enumerate((odeg, ideg)):
                    link(nc.vector.tensor_scalar(dg[:, k, :], deg[:, :], 1.0, None, ALU.min))
                    link(nc.vector.tensor_scalar(dmax[:, k, :], deg[:, :], 1.0, None, ALU.max))
                dve.sem_inc(t_sq, 1)
                dve.wait_ge(t_sq, 2)
                link(nc.vector.reciprocal(droot[:, :, :], droot[:, :, :]))
                link(nc.vector.tensor_tensor(dtmp[:, :, :], droot[:, :, :], droot[:, :, :], ALU.mult))
                link(nc.vector.tensor_tensor(dtmp[:, :, :], dtmp[:, :, :], dmax[:, :, :], ALU.mult))
                link(nc.vector.tensor_scalar(dtmp[:, :, :], dtmp[:, :, :], -0.5, 1.5, ALU.mult, ALU.add))
                link(nc.vector.tensor_tensor(droot[:, :, :], droot[:, :, :], dtmp[:, :, :], ALU.mult))
                link(nc.vector.scalar_tensor_tensor(out=scl[:, :, :], in0=droot[:, :, :], scalar=SCALE, in1=dg[:, :, :],
                                                    op0=ALU.mult, op1=ALU.mult))
                link(nc.vector.tensor_tensor(bias[0][:, :], bias[0][:, :], bias[1][:, :], ALU.add))
                link(nc.vector.tensor_scalar(bias[0][:, :], bias[0][:, :], 0.5, None, ALU.mult))

        layer0.close()
        yz = [whole.enter_context(nc.sbuf_tensor(f"yz{k}", [B, NB, 2 * D], F16)) for k in range(2)]
        chunks = [(c, min(4, NB - c)) for c in range(0, NB, 4)]
        with ExitStack() as scope:
            sb, ps = sb_in(scope), ps_in(scope)
            w1 = sb("w1", [D, D], F32)
            b1c = sb("b1c", [D, 1], F32)
            w2 = sb("w2", [D + 1, D], F32)
            CW = 4 * B
            h1 = [sb(f"h1{k}", [D + 1, CW], F32) for k in range(2)]
            norm = norm_buffers(sb, "m")
            xs = [sb(f"xs{k}", [B, 4, D], F32) for k in range(2)]
            ph = [bank(ps, f"ph{k}")[0:D, 0:CW] for k in range(2)]
            po = [bank(ps, f"po{k}")[0:B, :].rearrange("p (j f) -> p j f", j=4) for k in range(2)]
            s_w, s_h, s_hr, s_o, s_oa, s_v3, s_on, s_hi, s_lo = (sem("m_w"), sem("m_h"), sem("m_hr"), sem("m_o"), sem("m_oa"),
                                                                 sem("m_v"), sem("m_on"), sem("m_hi"), sem("m_lo"))
            s_sq, s_sr, s_nm, s_ap = sem("m_sq"), sem("m_sr"), sem("m_nm"), sem("m_ap")
            block = scope.enter_context(nc.Block())

            @block.sync
            def _(sp):
                sp.dma_start(w1[:, :], w1T).then_inc(s_w, 16)
                sp.dma_start(w2[:, :], w2T).then_inc(s_w, 16)
                sp.dma_start(b1c[:, :], b1).then_inc(s_w, 16)
                sp.wait_ge(s_w, 48)

            @block.gpsimd
            def _(pool):
                for k, (b0, nb) in enumerate(chunks):
                    pool.wait_ge(s_hi, k + 1)
                    if k >= 2:
                        pool.wait_ge(s_lo, 2 * k - 2)
                    for j in range(nb):
                        last = nc.gpsimd.tensor_scalar(xs[k % 2][:, j, :], X[:, b0 + j, :], scl[:, 1, b0 + j:b0 + j + 1], None, ALU.mult)
                    last.then_inc(s_lo, 1)
                    pool.wait_ge(s_lo, 2 * k + 1)
                    nc.gpsimd.tensor_tensor(yz[1][:, b0:b0 + nb, D:2 * D], xs[k % 2][:, 0:nb, :], yz[1][:, b0:b0 + nb, 0:D],
                                            ALU.subtract).then_inc(s_lo, 1)

            @block.tensor
            def _(pe):
                pe.wait_ge(s_w, 48)
                pe.wait_ge(s_on, 2)

                def up_product(k):
                    b0, nb = chunks[k]
                    if k >= 2:
                        pe.wait_ge(s_hr, k - 1)
                    nc.tensor.matmul(ph[k % 2][:, 0:nb * B], w1[:, :], acc[0:D, b0 * B:(b0 + nb) * B], start=True, stop=True).then_inc(s_h, 1)

                up_product(0)
                for k, (b0, nb) in enumerate(chunks):
                    if k + 1 < len(chunks):
                        up_product(k + 1)
                    pe.wait_ge(s_hr, k + 1)
                    if k >= 2:
                        pe.wait_ge(s_oa, k - 1)
                    for j in range(nb):
                        last = nc.tensor.matmul(po[k % 2][:, j, 0:D], h1[k % 2][:, j * B:(j + 1) * B], w2[:, :], start=True, stop=True)
                    last.then_inc(s_o, 1)

            @block.scalar
            def _(act):
                act.wait_ge(s_w, 48)

                def up_relu(k):
                    b0, nb = chunks[k]
                    act.wait_ge(s_h, k + 1)
                    if k >= 2:
                        act.wait_ge(s_o, k - 1)
                    nc.scalar.activation(h1[k % 2][0:D, 0:nb * B], ph[k % 2][:, 0:nb * B], ACT.Relu, bias=b1c[:, :]).then_inc(s_hr, 1)

                up_relu(0)
                for k, (b0, nb) in enumerate(chunks):
                    if k + 1 < len(chunks):
                        up_relu(k + 1)
                    apply_norm(nc, act, norm, X, k, b0, nb, s_sq, s_sr, s_nm, s_ap)
                    act.wait_ge(s_ap, k + 1)
                    for d in range(2):
                        for b in range(b0, b0 + nb):
                            last = nc.scalar.activation(yz[d][:, b, 0:D], X[:, b, :], ACT.Copy, scale=scl[:, d, b:b + 1])
                    last.then_inc(s_hi, 1)

            @block.vector
            def _(dve):
                made = [0]

                def link(ins):
                    made[0] += 1
                    ins.then_inc(s_v3, 1)
                    dve.wait_ge(s_v3, made[0])

                def low_halves(k):
                    b0, nb = chunks[k]
                    dve.wait_ge(s_hi, k + 1)
                    for d in range(1):
                        for b in range(b0, b0 + nb):
                            nc.vector.scalar_tensor_tensor(out=yz[d][:, b, D:2 * D], in0=X[:, b, :], scalar=scl[:, d, b:b + 1],
                                                           in1=yz[d][:, b, 0:D], op0=ALU.mult, op1=ALU.subtract)

                for k in range(2):
                    nc.vector.memset(h1[k][D:D + 1, :], 1.0).then_inc(s_on, 1)
                for k, (b0, nb) in enumerate(chunks):
                    dve.wait_ge(s_o, k + 1)
                    xb = X[:, b0:b0 + nb, :]
                    nc.vector.tensor_tensor(xb, xb, po[k % 2][:, 0:nb, 0:D], ALU.add).then_inc(s_oa, 1)
                    dve.wait_ge(s_oa, k + 1)
                    statistics(nc, dve, link, norm, X, k, b0, nb, s_sq)
                    if k:
                        low_halves(k - 1)
                    inverse_root(nc, dve, link, norm, k, b0, nb, s_sr, s_nm)
                low_halves(len(chunks) - 1)

        z, y = yz
        agt = whole.enter_context(nc.sbuf_tensor("agt", [D, N], F32))
        RING = 5
        PL = 1
        LEAD = 3
        START = 64
        with ExitStack() as scope:
            sb, ps = sb_in(scope), ps_in(scope)
            T = [sb(f"T{k}", [B, NB, SW], F16) for k in range(2)]
            sel = [sb(f"sel{k}", [P, 500], F16) for k in range(2)]
            goff_i = sb("goff_i", [P, 500], I32)
            goff = sb("goff", [P, 500], F32)
            tk = sb("tk", [P, 500], F32)
            keyt = sb("keyt", [P, NG, 2], F16)
            lot = sb("lot", [P, NG, 2], F16)
            keys = [sb(f"keys{k}", [P, 4 * PAIRS], F16) for k in range(2)]
            los = [sb(f"los{k}", [P, 4 * PAIRS], F16) for k in range(2)]
            yst = [sb(f"yst{k}", [B, 2, 2 * D], F16) for k in range(2)]
            KO = [sb(f"KO{k}", [P, 4, GW], F16) for k in range(RING)]
            LO = [sb(f"LO{k}", [P, 4, B], F16) for k in range(RING)]
            TX = [sb(f"TX{k}", [B, 2, 2, B], F16) for k in range(2)]
            pt = [bank(ps, f"pt{k}")[0:B, 0:2 * GW].rearrange("p (g n) -> p g n", g=2) for k in range(2)]
            px = [bank(ps, f"px{k}", F16)[0:B, 0:4 * P].rearrange("p (b h s) -> p b h s", b=2, h=2) for k in range(2)]
            pg = [bank(ps, f"pg{k}") for k in range(2)]
            pl = [bank(ps, f"pl{k}") for k in range(2)]
            pa = [b[0:D, 0:SW] for b in pl]
            g_zero = sem("g_zero")
            picked, multiplied, tabled, g_off, g_v = sem("picked"), sem("multiplied"), sem("tabled"), sem("g_off"), sem("g_v")
            staged = sem("staged")
            y_in = sem("y_in")
            hot = sem("hot")
            pool_hot = sem("pool_hot")
            built = sem("built")
            kept = sem("kept")
            turned = sem("turned")
            held = sem("held")
            summed = sem("summed")
            added = sem("c_added")
            at_done = sem("at_done")
            at_kept = sem("at_kept")
            widths = [(a, min(500, NG - a)) for a in range(0, NG, 500)]
            PICKS = len(widths) * 2 * TC
            RP = STRIPS * PAIRS
            block = scope.enter_context(nc.Block())

            def done(item):
                return item + (START + 1)

            def before(p):
                return {0: 1, 1: 3}.get(p, 2)

            def count(eng):
                return eng.value_load(rounds[0:1, 1:2], min_val=1, max_val=TT)

            def strips(eng, step):
                step(0, None, 0)
                with eng.Fori(0, (STRIPS - 3) // 2) as k:
                    step(eng.snap(k * 2 + 1), eng.snap(k * 2), 1)
                    step(eng.snap(k * 2 + 2), eng.snap(k * 2 + 1), 0)
                step(STRIPS - 2, STRIPS - 3, 1)
                step(STRIPS - 1, STRIPS - 2, 0)
                step(None, STRIPS - 1, 1)

            @block.gpsimd
            def _(pool):
                nc.gpsimd.iota(goff_i[:, :], pattern=[[GW, 500]], base=0, channel_multiplier=0).then_inc(g_off, 1)
                pool.sem_inc(y_in, START)
                pool.sem_inc(pool_hot, START)
                nc.gpsimd.memset(agt[:, :], 0.0).then_inc(g_zero, 1)
                nc.gpsimd.tensor_tensor(X[:, :, :], X[:, :, :], bias[0][:, :].unsqueeze(1).broadcast_to([B, NB, D]), ALU.add)
                with pool.Fori(0, count(pool)) as r:
                    def step(b, u, k):
                        if b is None:
                            return
                        lag = 1 if isinstance(b, int) and b == 0 else 2
                        hold(pool, carrier["pool"], summed, done(r * RP + (b * PAIRS - lag * PAIRS + PAIRS - 1)))
                        nc.gpsimd.tensor_copy(yst[k][:, :, :], y[:, bass.ds(b * 2, 2), :]).then_inc(y_in, 1)
                        b_at = pool.snap(r * RP + b * PAIRS)
                        hold(pool, carrier["pool"], staged, r * (2 * STRIPS) + (b * 2 + 2))
                        for p in range(PAIRS):
                            hold(pool, carrier["pool"], built, done(b_at + (p - RING)))
                            for m in range(4 - PL, 4):
                                last = nc.gpsimd.tensor_scalar(LO[p % RING][:, m, :], iota16[:, :], los[k][:, 4 * p + m:4 * p + m + 1],
                                                               None, ALU.is_equal)
                            last.then_inc(pool_hot, 1)
                    strips(pool, step)

            @block.tensor
            def _(pe):
                for s in (multiplied, built, turned, summed, at_done):
                    pe.sem_inc(s, START)
                with pe.Fori(0, count(pe)) as r:
                    pe.wait_ge(added, done(r * RP - 1))
                    pe.wait_ge(at_kept, done(r * STRIPS - 1))
                    for s in range(PICKS):
                        c, w = s % TC, widths[s // (2 * TC)][1]
                        pe.wait_ge(picked, done(r * PICKS + s))
                        if c == 0:
                            pe.wait_ge(tabled, done(r * (PICKS // TC) + (s // TC - 1)))
                        for table, to in ((da_te, pg[0]), (db_te, pg[1]), (lo_te, pl[0])):
                            last = nc.tensor.matmul(to[:, 0:w], table[:, c, :], sel[s % 2][:, 0:w], start=(c == 0), stop=(c == TC - 1))
                        last.then_inc(multiplied, 1)
                    pe.wait_ge(tabled, done(r * (PICKS // TC) + (PICKS // TC - 1)))

                    def step(b, u, k):
                        use = T[1 - k]
                        if b is not None:
                            b_at = pe.snap(r * RP + b * PAIRS)
                        if u is not None:
                            u_at = pe.snap(r * RP + u * PAIRS)
                            pe.wait_ge(kept, done(u_at + (PAIRS - 1)))

                        def sum_slot(p):
                            if p == 0:
                                pe.wait_ge(y_in, done(r * STRIPS + u))
                            pe.wait_ge(held, done(u_at + p))
                            pe.wait_ge(added, done(u_at + (p - before(p))))
                            for blk in range(2):
                                for part in range(2):
                                    last = nc.tensor.matmul(pg[p % 2][0:D, 0:SW], yst[1 - k][:, blk, part * D:(part + 1) * D],
                                                            TX[p % 2][:, blk, :, 0:B], start=(blk + part == 0), stop=(blk + part == 2))
                            last.then_inc(summed, 1)

                        for p in range(PAIRS):
                            if u is not None:
                                pe.wait_ge(held, done(u_at + (p - before(p))))
                                for blk in range(2):
                                    for h in range(2):
                                        last = nc.tensor.transpose(px[p % 2][:, blk, h, 0:B], use[:, 2 * p + h, blk * B:(blk + 1) * B],
                                                                   ident16[0:B, 0:B])
                                last.then_inc(turned, 1)
                            if b is not None:
                                pe.wait_ge(hot, done(b_at + p))
                                pe.wait_ge(pool_hot, done(b_at + p))
                                pe.wait_ge(kept, done(b_at + (p - before(p))))
                                for g in range(2):
                                    for j in range(2):
                                        last = nc.tensor.matmul(pt[p % 2][:, g, :], LO[p % RING][:, 2 * g + j, :],
                                                                KO[p % RING][:, 2 * g + j, :], start=(j == 0), stop=(j == 1))
                                last.then_inc(built, 1)
                            if u is not None:
                                if p == 0:
                                    pe.wait_ge(at_kept, done(r * STRIPS + u - 2))
                                for h in range(2):
                                    for part in range(2):
                                        last = nc.tensor.matmul(pa[1 - k][:, :], z[:, 2 * p + h, part * D:(part + 1) * D], use[:, 2 * p + h, :],
                                                                start=(p + h + part == 0), stop=(p == PAIRS - 1 and h + part == 2))
                                if p == PAIRS - 1:
                                    last.then_inc(at_done, 1)
                                if p:
                                    sum_slot(p - 1)
                        if u is not None:
                            sum_slot(PAIRS - 1)
                    strips(pe, step)

            @block.scalar
            def _(act):
                act.sem_inc(kept, START)
                act.sem_inc(held, START)
                with act.Fori(0, count(act)) as r:
                    def step(b, u, k):
                        if b is not None:
                            b_at = act.snap(r * RP + b * PAIRS)
                        if u is not None:
                            u_at = act.snap(r * RP + u * PAIRS)
                        for p in range(PAIRS):
                            if u is not None:
                                act.wait_ge(turned, done(u_at + p))
                                act.wait_ge(summed, done(u_at + (p - before(p))))
                                nc.scalar.activation(TX[p % 2][:, :, :, 0:B], px[p % 2][:, :, :, 0:B], ACT.Copy).then_inc(held, 1)
                            if b is not None:
                                act.wait_ge(built, done(b_at + p))
                                nc.scalar.activation(T[k][:, :, 2 * G * p:2 * G * (p + 1)].rearrange("s h (g d) -> s g h d", g=2),
                                                     pt[p % 2][:, :, :].rearrange("s g (h d) -> s g h d", h=NB), ACT.Copy).then_inc(kept, 1)
                    strips(act, step)

            @block.vector
            def _(dve):
                for s in (picked, tabled, hot, added, at_kept):
                    dve.sem_inc(s, START)
                dve.wait_ge(g_off, 1)
                nc.vector.tensor_copy(goff[:, :], goff_i[:, :]).then_inc(g_v, 1)
                nc.vector.memset(acc[0:D, 0:N], 0.0).then_inc(g_v, 1)
                dve.wait_ge(g_v, 2)
                dve.wait_ge(g_zero, 1)
                STEPS = 4 * (PICKS // TC) + 1
                with dve.Fori(0, count(dve)) as r:
                    v = [2]

                    def link(ins):
                        v[0] += 1
                        ins.then_inc(g_v, 1)
                        dve.wait_ge(g_v, r * STEPS + v[0])

                    for s in range(PICKS):
                        c, j, (a, w) = s % TC, s // TC % 2, widths[s // (2 * TC)]
                        dve.wait_ge(multiplied, done(r * PICKS + (s - 2)))
                        nc.vector.tensor_scalar(sel[s % 2][:, 0:w], t0row[:, a:a + w], tneg[:, c:c + 1], -float(j),
                                                ALU.add, ALU.is_equal).then_inc(picked, 1)
                        if c == TC - 1:
                            dve.wait_ge(multiplied, done(r * PICKS + s))
                            link(nc.vector.scalar_tensor_tensor(out=tk[:, 0:w], in0=pg[0][:, 0:w], scalar=8.0 * NB, in1=goff[:, 0:w],
                                                                op0=ALU.mult, op1=ALU.subtract))
                            link(nc.vector.tensor_tensor(tk[:, 0:w], tk[:, 0:w], pg[1][:, 0:w], ALU.add))
                            link(nc.vector.tensor_scalar(tk[:, 0:w], tk[:, 0:w], -float(GW * a), 0.0, ALU.add, ALU.max))
                            link(nc.vector.tensor_scalar(keyt[:, a:a + w, j], tk[:, 0:w], float(GW + 1), None, ALU.min))
                            nc.vector.tensor_copy(lot[:, a:a + w, j], pl[0][:, 0:w]).then_inc(tabled, 1)
                    hold(dve, carrier["dve"], tabled, done(r * (PICKS // TC) + (PICKS // TC - 1)))

                    def stage(b, k):
                        nc.vector.tensor_copy(keys[k][:, :].rearrange("p (g j) -> p g j", j=2),
                                              keyt[:, bass.ds(b * (2 * PAIRS), 2 * PAIRS), :]).then_inc(staged, 1)
                        nc.vector.tensor_copy(los[k][:, :].rearrange("p (g j) -> p g j", j=2),
                                              lot[:, bass.ds(b * (2 * PAIRS), 2 * PAIRS), :]).then_inc(staged, 1)
                        hold(dve, carrier["dve"], staged, r * (2 * STRIPS) + (b * 2 + 2))

                    def onehots(at, k, p):
                        dve.wait_ge(built, done(at + (p - RING)))
                        for m in range(4):
                            nc.vector.tensor_scalar(KO[p % RING][:, m, :], keytab[:, :], keys[k][:, 4 * p + m:4 * p + m + 1],
                                                    None, ALU.is_equal)
                        nc.vector.tensor_tensor(LO[p % RING][:, 0:4 - PL, :], iota16[:, :].unsqueeze(1).broadcast_to([P, 4 - PL, B]),
                                                los[k][:, 4 * p:4 * p + 4 - PL].unsqueeze(2).broadcast_to([P, 4 - PL, B]),
                                                ALU.is_equal).then_inc(hot, 1)

                    def step(b, u, k):
                        if b is not None:
                            b_at = dve.snap(r * RP + b * PAIRS)
                        if u is not None:
                            u_at = dve.snap(r * RP + u * PAIRS)
                        first_strip, last_strip = isinstance(b, int) and b == 0, isinstance(b, int) and b == STRIPS - 1
                        if first_strip:
                            stage(b, k)
                            for p in range(LEAD):
                                onehots(b_at, k, p)

                        def add_slot(p):
                            dve.wait_ge(summed, done(u_at + p))
                            dve.wait_ge(added, done(u_at + (p - PAIRS)))
                            a = acc[0:D, SW * p:SW * (p + 1)]
                            nc.vector.tensor_tensor(a, a, pg[p % 2][0:D, 0:SW], ALU.add).then_inc(added, 1)

                        for p in range(PAIRS):
                            if u is not None and p >= 2:
                                add_slot(p - 2)
                            if b is not None and p + LEAD < PAIRS:
                                onehots(b_at, k, p + LEAD)
                            elif b is not None and not last_strip:
                                if p + LEAD == PAIRS:
                                    stage(b + 1, 1 - k)
                                onehots(b_at + PAIRS, 1 - k, p + LEAD - PAIRS)
                        if u is not None:
                            add_slot(PAIRS - 2)
                            add_slot(PAIRS - 1)
                            dve.wait_ge(at_done, done(r * STRIPS + u))
                            dve.wait_ge(at_kept, done(r * STRIPS + u - 1))
                            a = agt[:, bass.ds(u * SW, SW)]
                            nc.vector.tensor_tensor(a, a, pa[1 - k][:, :], ALU.add).then_inc(at_kept, 1)
                    strips(dve, step)
                    nc.vector.tensor_scalar(t0row[:, :], t0row[:, :], 2.0, None, ALU.add).then_inc(g_v, 1)
                    hold(dve, carrier["dve"], g_v, r * STEPS + (2 + STEPS))

        with ExitStack() as scope:
            sb, ps = sb_in(scope), ps_in(scope)
            wsd = sb("wsd", [D, D], F32)
            wds = sb("wds", [D, D], F32)
            coef = sb("coef", [B, 2, NB], F32)
            norm = norm_buffers(sb, "f")
            pf = [[bank(ps, f"pf{k}{d}")[0:B, :].rearrange("p (j f) -> p j f", j=4) for d in range(2)] for k in range(2)]
            f_w, f_p, f_a, f_v, f_out = sem("f_w"), sem("f_p"), sem("f_a"), sem("f_v"), sem("f_out")
            f_sq, f_sr, f_nm, f_ap = sem("f_sq"), sem("f_sr"), sem("f_nm"), sem("f_ap")
            block = scope.enter_context(nc.Block())

            @block.sync
            def _(sp):
                sp.dma_start(wsd[:, :], wsdT).then_inc(f_w, 16)
                sp.dma_start(wds[:, :], wdsT).then_inc(f_w, 16)
                ob = out.rearrange("(b p) f -> p b f", p=B)
                for k, (b0, nb) in enumerate(chunks):
                    sp.wait_ge(f_ap, k + 1)
                    sp.dma_start(ob[:, b0:b0 + nb, :], X[:, b0:b0 + nb, :]).then_inc(f_out, 16)
                sp.wait_ge(f_out, 16 * len(chunks))

            @block.tensor
            def _(pe):
                pe.wait_ge(f_w, 32)
                for k, (b0, nb) in enumerate(chunks):
                    if k >= 2:
                        pe.wait_ge(f_a, 2 * k - 2)
                    for d, (src, w) in enumerate(((acc, wsd), (agt, wds))):
                        for j in range(nb):
                            last = nc.tensor.matmul(pf[k % 2][d][:, j, 0:D], src[0:D, (b0 + j) * B:(b0 + j + 1) * B], w[:, :],
                                                    start=True, stop=True)
                    last.then_inc(f_p, 1)

            @block.scalar
            def _(act):
                for k, (b0, nb) in enumerate(chunks):
                    apply_norm(nc, act, norm, X, k, b0, nb, f_sq, f_sr, f_nm, f_ap)

            @block.vector
            def _(dve):
                made = [0]

                def link(ins):
                    made[0] += 1
                    ins.then_inc(f_v, 1)
                    dve.wait_ge(f_v, made[0])

                link(nc.vector.tensor_scalar(coef[:, :, :], scl[:, :, :], 0.5 / SCALE / SCALE, None, ALU.mult))
                for k, (b0, nb) in enumerate(chunks):
                    dve.wait_ge(f_p, k + 1)
                    for d in range(2):
                        for j in range(nb):
                            b = b0 + j
                            last = nc.vector.scalar_tensor_tensor(out=X[:, b, :], in0=pf[k % 2][d][:, j, 0:D], scalar=coef[:, d, b:b + 1],
                                                                  in1=X[:, b, :], op0=ALU.mult, op1=ALU.add)
                        last.then_inc(f_a, 1)
                        dve.wait_ge(f_a, 2 * k + d + 1)
                    statistics(nc, dve, link, norm, X, k, b0, nb, f_sq)
                    if k:
                        b1_, nb1 = chunks[k - 1]
                        inverse_root(nc, dve, link, norm, k - 1, b1_, nb1, f_sr, f_nm)
                inverse_root(nc, dve, link, norm, len(chunks) - 1, *chunks[-1], f_sr, f_nm)


def kernel(x, src, dst, edge_attr_96, L0_gnn_W_edge, L0_gnn_b_edge, L0_gnn_eps, L0_gnn_W1, L0_gnn_b1, L0_gnn_W2, L0_gnn_b2,
           L1_gnn_W_sd, L1_gnn_b_sd, L1_gnn_W_ds, L1_gnn_b_ds):
    import numpy as np
    import concourse.bacc as bacc
    from concourse.bass_utils import run_bass_kernel_spmd

    def padded(a, fill, n):
        out = np.full((n,), fill, np.int32)
        out[:E] = np.asarray(a)
        return out

    def by_tile(a):
        return np.ascontiguousarray(padded(a, N, TT * P).reshape(TC, P, P).transpose(1, 0, 2).reshape(P, TT))

    def by_edge(a):
        return np.ascontiguousarray(padded(a, N, TILES * P).reshape(TILES, P).T)

    def with_bias(w, b):
        return np.ascontiguousarray(np.concatenate([np.asarray(w).T, np.asarray(b)[None, :]], axis=0))

    x = np.ascontiguousarray(x)
    ea = np.zeros((D, TILES * P), np.float32)
    ea[:, :E] = np.asarray(edge_attr_96).T
    arrays = {
        "x": x,
        "xT": np.ascontiguousarray(x.T),
        "dst_te": by_tile(dst), "src_te": by_tile(src),
        "dst_et": by_edge(dst), "src_et": by_edge(src),
        "src_gather": np.ascontiguousarray(padded(src, 0, TILES * P).reshape(2 * CH, HT, P).transpose(0, 2, 1)),
        "eaT": ea,
        "weT": with_bias(L0_gnn_W_edge, L0_gnn_b_edge),
        "w1T": np.ascontiguousarray(np.asarray(L0_gnn_W1).T),
        "b1": np.ascontiguousarray(L0_gnn_b1).reshape(D, 1),
        "w2T": with_bias(L0_gnn_W2, L0_gnn_b2),
        "eps": np.ascontiguousarray(L0_gnn_eps).reshape(1, 1),
        "wsdT": np.ascontiguousarray(np.asarray(L1_gnn_W_sd).T),
        "wdsT": np.ascontiguousarray(np.asarray(L1_gnn_W_ds).T),
        "bsd": np.ascontiguousarray(L1_gnn_b_sd).reshape(1, D),
        "bds": np.ascontiguousarray(L1_gnn_b_ds).reshape(1, D),
    }
    nc = bacc.Bacc("TRN2", target_bir_lowering=False, num_devices=1)
    args = [nc.dram_tensor("in_" + k, a.shape, mybir.dt.from_np(a.dtype), kind="ExternalInput").ap() for k, a in arrays.items()]
    out = nc.dram_tensor("out", (N, D), F32, kind="ExternalOutput").ap()
    gnn(nc, *args, out)
    result = run_bass_kernel_spmd(nc, [{"in_" + k: a for k, a in arrays.items()}], core_ids=[0])
    return result.results[0]["out"]
```

```python
from contextlib import ExitStack

import concourse.bass as bass
from concourse import mybir

F32, F16, I32 = mybir.dt.float32, mybir.dt.float16, mybir.dt.int32
ALU, ACT, AX = mybir.AluOpType, mybir.ActivationFunctionType, mybir.AxisListType

N, E, D = 6250, 100000, 96
P = 128
B = 125
NB = N // B
HT = 8
CH = -(-E // (2 * HT * P))
TILES = 2 * HT * CH
TC = -(-TILES // P)
TT = TC * P
W = 64
ACCW = N + W + 6
G = 5
NG = N // G
GC = -(-NG // P)
GW = G * NB
PAIRS = 25
STRIPS = NG // (2 * PAIRS)
SW = 2 * B
STEP = 8
NEAR = (TT * P - P) // STEP + 1
SCALE = 1024.0
EPS = 1e-5


def bank(ps, name, dt=F32):
    return ps(name, [P, 512 if dt == F32 else 1024], dt)


def hold(eng, carrier, sem, value):
    eng.wait_ge(sem, value)
    eng.sem_inc(carrier, 1)


def norm_buffers(sb, tag):
    return [sb(f"{tag}_{n}", [B, NB, w], F32) for n, w in (("stats", 6), ("mv", 2), ("var", 1), ("inv", 1), ("off", 1), ("tmp", 1))]


def statistics(nc, dve, link, norm, X, k, b0, nb, s_sq):
    stats, mv, var = norm[:3]
    for b in range(b0, b0 + nb):
        last = nc.vector.bn_stats(stats[:, b, :], X[:, b, :])
    link(last)
    for b in range(b0, b0 + nb):
        last = nc.vector.bn_aggr(mv[:, b, :], stats[:, b, :])
    link(last)
    nc.vector.tensor_scalar(var[:, b0:b0 + nb, 0], mv[:, b0:b0 + nb, 1], EPS, None, ALU.add).then_inc(s_sq, 1)


def inverse_root(nc, dve, link, norm, k, b0, nb, s_sr, s_nm):
    _, mv, var, inv, off, tmp = norm
    v, i, o, t = (a[:, b0:b0 + nb, 0] for a in (var, inv, off, tmp))
    dve.wait_ge(s_sr, k + 1)
    link(nc.vector.reciprocal(i, i))
    link(nc.vector.tensor_tensor(t, i, i, ALU.mult))
    link(nc.vector.tensor_tensor(t, t, v, ALU.mult))
    link(nc.vector.tensor_scalar(t, t, -0.5, 1.5, ALU.mult, ALU.add))
    link(nc.vector.tensor_tensor(i, i, t, ALU.mult))
    nc.vector.scalar_tensor_tensor(out=o, in0=mv[:, b0:b0 + nb, 0], scalar=-1.0, in1=i, op0=ALU.mult, op1=ALU.mult).then_inc(s_nm, 1)


def root(nc, act, norm, k, b0, nb, s_sq, s_sr):
    act.wait_ge(s_sq, k + 1)
    nc.scalar.activation(norm[3][:, b0:b0 + nb, 0], norm[2][:, b0:b0 + nb, 0], ACT.Sqrt).then_inc(s_sr, 1)


def apply_norm(nc, act, norm, X, k, b0, nb, s_nm, s_ap):
    act.wait_ge(s_nm, k + 1)
    for b in range(b0, b0 + nb):
        last = nc.scalar.activation(X[:, b, :], X[:, b, :], ACT.Identity, bias=norm[4][:, b, :], scale=norm[3][:, b, :])
    last.then_inc(s_ap, 1)


def gnn(nc, x, xT, dst_t, near, dst_et, src_et, src_gather, eaT, weT, w1T, b1, w2T, eps, wsdT, wdsT, bsd, bds, out):
    nc.disable_value_cache = True
    whole = ExitStack()

    def sb_in(scope):
        return lambda name, shape, dt: scope.enter_context(nc.sbuf_tensor(name, shape, dt))

    def ps_in(scope):
        return lambda name, shape, dt: scope.enter_context(nc.psum_tensor(name, shape, dt))

    def sem(name):
        return whole.enter_context(nc.semaphore(name))

    with whole:
        sb = sb_in(whole)
        carrier = {e: sem(f"carrier_{e}") for e in ("pool", "dve")}
        acc = sb("acc", [P, max(ACCW, NB * 2 * D)], F32)
        X = sb("X", [B, NB, D], F32)
        rounds = sb("rounds", [1, 2], I32)
        nidx = sb("nidx", [P, GC], I32)
        thr = sb("thr", [P, 2, GC], F32)
        mask = sb("mask", [P, GC], F32)
        tile_f = sb("tile_f", [P, 2, GC], F32)
        tile_i = sb("tile_i", [P, 2, GC], I32)
        ruler = sb("ruler", [P, 2, P], F32)
        ones = sb("ones", [P, P], F32)
        rnf = sb("rnf", [1, 2], F32)
        rni = sb("rni", [1, 2], I32)
        iota16 = sb("iota16", [P, B], F16)
        keytab = sb("keytab", [P, GW], F16)
        ident = sb("ident", [P, P], F32)
        ident16 = sb("ident16", [P, P], F16)
        odeg = sb("odeg", [B, NB], F32)
        ideg = sb("ideg", [B, NB], F32)
        scl = sb("scl", [B, 2, NB], F32)
        coef = sb("coef", [B, 2, NB], F32)
        bias = [sb(f"bias{k}", [B, D], F32) for k in range(2)]

        layer0 = ExitStack()
        sb = sb_in(layer0)
        dloc = sb("dloc", [P, TILES], F32)
        hi_et = sb("hi_et", [P, TILES], F16)
        lo_et = sb("lo_et", [P, TILES], F16)
        iotaw = sb("iotaw", [P, W], F32)
        first = sb("first", [1, TILES // 4], I32)
        qmin = sb("qmin", [P, TILES // 4], F32)
        qmax = sb("qmax", [1, TILES // 4], F32)
        di = sb("di", [P, TT], I32)
        qi = sb("qi", [P, TILES], I32)
        wide = sb("wide", [P, 4, P], F32)
        cols = sb("cols", [P, 2 * TC], F32)
        row = sb("row", [P, 2 * TC, P], F32)
        up_i = sb("up_i", [P, TT], I32)
        up = sb("up", [P, TT], F32)
        down = sb("down", [P, TT], F32)
        reach = [sb(f"reach{k}", [P, TT], F32) for k in range(2)]
        thr_i = sb("thr_i", [P, GC], I32)
        ends = sb("ends", [P, 2, GC], F32)
        we = sb("we", [D + 1, D], F32)
        ea = [sb(f"ea{h}", [D + 1, HT * P], F32) for h in range(2)]
        idx = [sb(f"idx{h}", [P, HT], I32) for h in range(2)]
        msg = [sb(f"msg{k}", [P, 4, D + 1], F32) for k in range(4)]
        s_we, s_one = sem("s_we"), sem("s_one")
        X_BLOCKS = 10
        s_x2 = [sem(f"s_x2{b}") for b in range(0, NB, X_BLOCKS)]
        ea_in = [sem(f"ea_in{h}") for h in range(2)]
        idx_in = [sem(f"idx_in{h}") for h in range(2)]
        xg_in = [sem(f"xg_in{k}") for k in range(4)]

        def load_sources(sp, h, i):
            sp.dma_start(idx[h][:, :], src_gather[bass.ds(i * 2 + h, 1), :, :].rearrange("a p t -> (a p) t")).then_inc(idx_in[h], 16)

        def load_attributes(sp, h, i):
            sp.dma_start(ea[h][0:D, :], eaT[:, bass.ds(i * (2 * HT * P) + h * HT * P, HT * P)]).then_inc(ea_in[h], 16)

        def gather_sources(k):
            h, q = divmod(k, 2)
            for j in range(4):
                nc.gpsimd.indirect_dma_start(out=msg[k][:, j, 0:D], out_offset=None, in_=x[:, :],
                                             in_offset=bass.IndirectOffsetOnAxis(ap=idx[h][:, 4 * q + j:4 * q + j + 1], axis=0)
                                             ).then_inc(xg_in[k], 16)

        tmin = row[:, 0:TC, :].rearrange("p c t -> p (c t)")
        tmax = row[:, TC:2 * TC, :].rearrange("p c t -> p (c t)")

        def high(dve, link, s, q):
            link(nc.vector.tensor_scalar(q, s, 8389.0, None, ALU.mult))
            link(nc.vector.tensor_scalar(q, q, 20, None, ALU.arith_shift_right))

        def rows(dve, link, k0, k1, s_wide, s_row, pr):
            for k in range(k0, k1):
                if k - k0 >= 4:
                    dve.wait_ge(s_row, k - k0 - 3)
                nc.vector.tensor_scalar(wide[:, k % 4, :], ones[:, :], cols[:, k:k + 1], None, ALU.mult).then_inc(s_wide, 1)
            for n, k in enumerate(range(k0, k1, 4)):
                m = min(4, k1 - k)
                dve.wait_ge(s_row, k - k0 + m)
                link(nc.vector.tensor_copy(row[:, k:k + m, :], pr[n][:, 0:m, :]))

        def row_products(pe, k0, k1, s_wide, s_row, pr):
            for k in range(k0, k1):
                pe.wait_ge(s_wide, k - k0 + 1)
                nc.tensor.matmul(pr[(k - k0) // 4][:, (k - k0) % 4, :], wide[:, k % 4, :], ident[:, :],
                                 start=True, stop=True).then_inc(s_row, 1)

        with ExitStack() as scope:
            sb, ps = sb_in(scope), ps_in(scope)
            dei = sb("dei", [P, TILES], I32)
            sei = sb("sei", [P, TILES], I32)
            key_i = sb("key_i", [P, GW], I32)
            zero = sb("zero", [P, 1], F32)
            s_zero = sem("s_zero")
            epsc = sb("epsc", [D, 1], F32)
            eps1 = sb("eps1", [D, 1], F32)
            pr = [ps(f"pr{i}", [P, 4, P], F32) for i in range(4)]
            s_di, s_dei, s_sei, s_x, s_eps, s_b = sem("s_di"), sem("s_dei"), sem("s_sei"), sem("s_x"), sem("s_eps"), sem("s_b")
            s_const, s_id, s_wide, s_row, s_v, s_e1, s_acc = (sem("s_const"), sem("s_id"), sem("s_wide"), sem("s_row"),
                                                              sem("s_v"), sem("s_e1"), sem("s_acc"))
            block = scope.enter_context(nc.Block())

            @block.sync
            def _(sp):
                for h in range(2):
                    load_sources(sp, h, 0)
                sp.dma_start(di[:, :].rearrange("p (c e) -> p c e", c=TC), dst_t.rearrange("(c p) e -> p c e", p=P)).then_inc(s_di, 16)
                sp.dma_start(sei[:, :], src_et).then_inc(s_sei, 16)
                sp.dma_start(dei[:, :], dst_et).then_inc(s_dei, 16)
                sp.dma_start(we[:, :], weT).then_inc(s_we, 16)
                sp.dma_start(epsc[:, :], eps.broadcast_to([D, 1])).then_inc(s_eps, 16)
                sp.dma_start(acc[0:D, 0:N], xT).then_inc(s_x, 16)
                sp.dma_start(bias[0][:, :], bsd.broadcast_to([B, D])).then_inc(s_b, 16)
                sp.dma_start(bias[1][:, :], bds.broadcast_to([B, D])).then_inc(s_b, 16)
                for h in range(2):
                    load_attributes(sp, h, 0)
                sp.wait_ge(s_b, 32)

            @block.gpsimd
            def _(pool):
                nc.gpsimd.memset(ident[:, :], 0.0).then_inc(s_id, 1)
                nc.gpsimd.memset(ident16[:, :], 0.0).then_inc(s_id, 1)
                nc.gpsimd.memset(ones[:, :], 1.0).then_inc(s_const, 1)
                pool.wait_ge(s_id, 2)
                for m in (ident, ident16):
                    nc.gpsimd.affine_select(out=m[:, :], in_=m[:, :], compare_op=ALU.not_equal, fill=1.0, base=0,
                                            pattern=[[-1, P]], channel_multiplier=1).then_inc(s_id, 1)
                nc.gpsimd.iota(up_i[:, :], pattern=[[1, TT]], base=0, channel_multiplier=0).then_inc(s_const, 1)
                nc.gpsimd.iota(thr_i[:, :], pattern=[[G * P, GC]], base=0, channel_multiplier=G).then_inc(s_const, 1)
                nc.gpsimd.iota(key_i[:, :], pattern=[[1, NB], [NB, G]], base=1, channel_multiplier=0).then_inc(s_const, 1)
                for k in range(4):
                    if k % 2 == 0:
                        pool.wait_ge(idx_in[k // 2], 16)
                    gather_sources(k)

            @block.tensor
            def _(pe):
                pe.wait_ge(s_id, 4)
                row_products(pe, 0, 2 * TC, s_wide, s_row, pr)

            @block.scalar
            def _(act):
                act.wait_ge(s_zero, 1)
                nc.scalar.activation(acc[D:D + 1, 0:ACCW], zero[D:D + 1, :].broadcast_to([1, ACCW]), ACT.Copy)
                act.wait_ge(s_eps, 16)
                nc.scalar.activation(eps1[:, :], epsc[:, :], ACT.Copy, bias=1.0).then_inc(s_e1, 1)
                act.wait_ge(s_e1, 1)
                act.wait_ge(s_x, 16)
                nc.scalar.activation(acc[0:D, 0:N], acc[0:D, 0:N], ACT.Copy, scale=eps1[:, :]).then_inc(s_acc, 1)

            @block.vector
            def _(dve):
                made = [0]

                def link(ins):
                    made[0] += 1
                    ins.then_inc(s_v, 1)
                    dve.wait_ge(s_v, made[0])

                nc.vector.memset(acc[0:D, N:ACCW], 0.0)
                nc.vector.memset(zero[:, :], 0.0).then_inc(s_zero, 1)
                for h in range(2):
                    nc.vector.memset(ea[h][D:D + 1, :], 1.0).then_inc(s_one, 1)
                for k in range(4):
                    nc.vector.memset(msg[k][:, :, D:D + 1], 1.0)
                dve.wait_ge(s_di, 16)
                for k, op in enumerate((ALU.min, ALU.max)):
                    link(nc.vector.tensor_reduce(cols[:, k * TC:(k + 1) * TC], di[:, :].rearrange("p (c e) -> p c e", c=TC), AX.X, op))
                dve.wait_ge(s_const, 1)
                rows(dve, link, 0, 2 * TC, s_wide, s_row, pr)
                dve.wait_ge(s_sei, 16)
                q = qi[:, :]
                high(dve, link, sei[:, :], q)
                nc.vector.tensor_copy(hi_et[:, :], q)
                nc.vector.scalar_tensor_tensor(out=lo_et[:, :], in0=q, scalar=-float(B), in1=sei[:, :], op0=ALU.mult, op1=ALU.add)
                dve.wait_ge(s_dei, 16)
                link(nc.vector.tensor_reduce(qmin[:, :], tmin[:, 0:TILES].rearrange("p (q j) -> p q j", j=4), AX.X, ALU.min))
                link(nc.vector.tensor_reduce(qmax[:, :], tmax[0:1, 0:TILES].rearrange("p (q j) -> p q j", j=4), AX.X, ALU.max))
                nc.vector.tensor_tensor(dloc[:, :].rearrange("p (q j) -> p q j", j=4), dei[:, :].rearrange("p (q j) -> p q j", j=4),
                                        qmin[:, :].unsqueeze(2).broadcast_to([P, TILES // 4, 4]), ALU.subtract)
                nc.vector.tensor_copy(first[:, :], qmin[0:1, :])
                dve.wait_ge(s_const, 4)
                nc.vector.tensor_copy(iota16[:, :], up_i[:, 0:B])
                nc.vector.tensor_copy(iotaw[:, :], up_i[:, 0:W])
                nc.vector.tensor_copy(keytab[:, :], key_i[:, :])
                nc.vector.tensor_copy(thr[:, 0, :], thr_i[:, :])
                nc.vector.tensor_scalar(thr[:, 1, :], thr_i[:, :], float(G - 1), None, ALU.add)
                nc.vector.tensor_scalar(mask[:, :], thr_i[:, :], float(N), None, ALU.is_lt)
                nc.vector.tensor_scalar(down[:, :], up_i[:, :], -1.0, float(TT), ALU.mult, ALU.add)
                nc.vector.tensor_scalar(up[:, :], up_i[:, :], 1.0, None, ALU.add)
                link(nc.vector.tensor_tensor(qmax[:, :], qmax[:, :], qmin[0:1, :], ALU.subtract))
                nc.vector.tensor_copy(ruler[:, 0, :], down[:, TT - P:TT])
                nc.vector.tensor_copy(ruler[:, 1, :], up[:, 0:P])
                link(nc.vector.tensor_reduce(rnf[:, 0:1], qmax[:, :], AX.X, ALU.max))
                link(nc.vector.tensor_scalar(rni[:, 0:1], rnf[:, 0:1], float(W), None, ALU.add))
                link(nc.vector.tensor_scalar(rounds[:, 0:1], rni[:, 0:1], W.bit_length() - 1, None, ALU.arith_shift_right))

        with ExitStack() as scope:
            sb, ps = sb_in(scope), ps_in(scope)
            win = [sb(f"win{q}", [P, 4, W], F32) for q in range(2)]
            lo1 = [sb(f"lo1{q}", [P, 4, B], F16) for q in range(2)]
            hi1 = [sb(f"hi1{q}", [P, 4, NB], F16) for q in range(2)]
            pm = [bank(ps, f"pm{q}")[:, 0:4 * D].rearrange("p (j f) -> p j f", j=4) for q in range(2)]
            pw = [bank(ps, f"pw{q}")[0:D + 1, 0:W] for q in range(2)]
            pd = [bank(ps, f"pd{h}")[0:B, 0:NB] for h in range(2)]
            CREDIT = 2
            prod_done = [sem(f"prod_done{q}") for q in range(2)]
            sum_done = [sem(f"sum_done{q}") for q in range(2)]
            relu_done = [sem(f"relu_done{q}") for q in range(2)]
            hot_done = [sem(f"hot_done{q}") for q in range(2)]
            seg_done = [sem(f"seg_done{q}") for q in range(2)]
            added, s_rnd = sem("added"), sem("s_rnd")
            block = scope.enter_context(nc.Block())

            def count(eng):
                return eng.value_load(rounds[0:1, 0:1], min_val=1, max_val=N)

            def quarter(n, h):
                return n * 2 + (h + 1 + CREDIT)

            @block.sync
            def _(sp):

                def step(r, i):
                    n = sp.snap(r * CH + i)
                    for h in range(2):
                        for q in range(2):
                            sp.wait_ge(xg_in[2 * h + q], n * 64)
                        load_sources(sp, h, i)
                        sp.wait_ge(prod_done[1], quarter(n - 1, h))
                        load_attributes(sp, h, i)

                rnds = count(sp)
                with sp.Fori(0, rnds) as r:
                    with sp.Fori(1, CH) as i:
                        step(r, i)
                    with sp.If(sp.snap(rnds - r - 1)):
                        step(sp.snap(r + 1), 0)

            @block.gpsimd
            def _(pool):
                def step(r, i):
                    n = pool.snap(r * CH + i)
                    for h in range(2):
                        hold(pool, carrier["pool"], idx_in[h], n * 16 + 16)
                        for q in range(2):
                            hold(pool, carrier["pool"], seg_done[q], quarter(n - 1, h))
                            gather_sources(2 * h + q)

                rnds = count(pool)
                with pool.Fori(0, rnds) as r:
                    with pool.Fori(1, CH) as i:
                        step(r, i)
                    with pool.If(pool.snap(rnds - r - 1)):
                        step(pool.snap(r + 1), 0)

            @block.tensor
            def _(pe):
                for s in prod_done + seg_done:
                    pe.sem_inc(s, CREDIT)
                pe.wait_ge(s_we, 16)
                pe.wait_ge(s_one, 2)
                with pe.Fori(0, count(pe)) as r:
                    with pe.Fori(0, CH) as i:
                        n = pe.snap(r * CH + i)

                        def products(k):
                            h, q = divmod(k, 2)
                            if q == 0:
                                pe.wait_ge(ea_in[h], n * 16 + 16)
                            for j in range(4):
                                t = 4 * q + j
                                last = nc.tensor.matmul(pm[q][:, j, :], ea[h][:, t * P:(t + 1) * P], we[:, :], start=True, stop=True)
                            last.then_inc(prod_done[q], 1)

                        def segments(k):
                            h, q = divmod(k, 2)
                            pe.wait_ge(relu_done[q], quarter(n, h))
                            pe.wait_ge(hot_done[q], quarter(n, h))
                            for j in range(4):
                                nc.tensor.matmul(pw[q], msg[k][:, j, :], win[q][:, j, :], start=(j == 0), stop=(j == 3))
                            for j in range(4):
                                last = nc.tensor.matmul(pd[h][:, :], lo1[q][:, j, :], hi1[q][:, j, :],
                                                        start=(q == 0 and j == 0), stop=(q == 1 and j == 3))
                            last.then_inc(seg_done[q], 1)

                        products(0)
                        for k in range(1, 4):
                            products(k)
                            segments(k - 1)
                        segments(3)

            @block.scalar
            def _(act):
                for s in relu_done:
                    act.sem_inc(s, CREDIT)
                with act.Fori(0, count(act)) as r:
                    with act.Fori(0, CH) as i:
                        n = act.snap(r * CH + i)
                        for k in range(4):
                            act.wait_ge(sum_done[k % 2], quarter(n, k // 2))
                            nc.scalar.activation(msg[k][:, :, 0:D], msg[k][:, :, 0:D], ACT.Relu).then_inc(relu_done[k % 2], 1)

            @block.vector
            def _(dve):
                for s in sum_done + hot_done:
                    dve.sem_inc(s, CREDIT)
                regs = [dve.alloc_register(f"first_node{k}") for k in range(4)]

                def steps(r, i, beside=None):
                    n = dve.snap(r * CH + i)
                    dve.load(regs, first[0:1, bass.ds(i * 4, 4)])
                    node = [dve.snap(g, min_val=0, max_val=N) for g in regs]

                    def onehots(k):
                        t0, q = i * (2 * HT) + 4 * k, k % 2
                        for table, ruler, hot, w in ((dloc, iotaw, win, W), (lo_et, iota16, lo1, B), (hi_et, iota16, hi1, NB)):
                            last = nc.vector.tensor_tensor(
                                hot[q][:, :, :], ruler[:, 0:w].unsqueeze(1).broadcast_to([P, 4, w]),
                                table[:, bass.ds(t0, 4)].unsqueeze(2).broadcast_to([P, 4, w]), ALU.is_equal)
                        last.then_inc(hot_done[q], 1)

                    def add_source(k):
                        dve.wait_ge(prod_done[k % 2], quarter(n, k // 2))
                        dve.wait_ge(xg_in[k], n * 64 + 64)
                        nc.vector.tensor_tensor(msg[k][:, :, 0:D], msg[k][:, :, 0:D], pm[k % 2][:, :, :], ALU.add).then_inc(sum_done[k % 2], 1)

                    def accumulate(k):
                        h, q = divmod(k, 2)
                        dve.wait_ge(seg_done[q], quarter(n, h))
                        a = acc[0:D + 1, bass.ds(node[k], W)]
                        nc.vector.tensor_tensor(a, a, pw[q], ALU.add).then_inc(added, 1)
                        hold(dve, carrier["dve"], added, n * 6 + (k + 1 + h))
                        if q:
                            nc.vector.tensor_tensor(odeg[:, :], odeg[:, :], pd[h][:, :], ALU.add).then_inc(added, 1)
                            hold(dve, carrier["dve"], added, n * 6 + 3 * (h + 1))

                    onehots(0)
                    add_source(0)
                    for k in range(1, 4):
                        onehots(k)
                        add_source(k)
                        accumulate(k - 1)
                        if beside and k == 2:
                            beside()
                    accumulate(3)

                with dve.Fori(0, count(dve)) as r:
                    EV = 3 + 4 * GC
                    nc.vector.memset(odeg[:, :], 0.0).then_inc(s_rnd, 1)
                    hold(dve, carrier["dve"], s_rnd, r * EV + 1)
                    with dve.Fori(0, GC) as c:
                        v = r * EV + c * 4

                        def ends_part(part):
                            e, pick = divmod(part, 2)
                            tiles, op, ruler = ((tmax, ALU.is_ge, down), (tmin, ALU.is_le, up))[e]
                            if pick:
                                hold(dve, carrier["dve"], s_rnd, v + (2 * e + 2))
                                nc.vector.tensor_reduce(ends[:, e, bass.ds(c, 1)], reach[e][:, :], AX.X, ALU.max).then_inc(s_rnd, 1)
                            else:
                                nc.vector.scalar_tensor_tensor(out=reach[e][:, :], in0=tiles, scalar=thr[:, e, bass.ds(c, 1)], in1=ruler[:, :],
                                                               op0=op, op1=ALU.mult).then_inc(s_rnd, 1)

                        for part in range(4):
                            steps(r, dve.snap(c * 4 + part), lambda: ends_part(part))
                        hold(dve, carrier["dve"], s_rnd, v + 5)
                    done = [4 * GC + 1]

                    def link(ins):
                        done[0] += 1
                        ins.then_inc(s_rnd, 1)
                        dve.wait_ge(s_rnd, r * EV + done[0])

                    with dve.Fori(4 * GC, CH) as i:
                        steps(r, i)
                    link(nc.vector.tensor_scalar(dloc[:, :], dloc[:, :], float(W), None, ALU.subtract))
                    nc.vector.tensor_scalar(first[:, :], first[:, :], float(W), float(N), ALU.add, ALU.min).then_inc(s_rnd, 1)
                    done[0] += 1
                    hold(dve, carrier["dve"], s_rnd, r * EV + done[0])
                    assert done[0] == EV, (done, EV)

        with ExitStack() as scope:
            ps = ps_in(scope)
            pdeg = bank(ps, "pdeg")
            t_v, t_deg, t_sq, t_din = sem("t_v"), sem("t_deg"), sem("t_sq"), sem("t_din")
            deg_rows = layer0.enter_context(nc.sbuf_tensor("deg_rows", [NB, B], F32))
            dg = layer0.enter_context(nc.sbuf_tensor("dg", [B, 2, NB], F32))
            dmax = layer0.enter_context(nc.sbuf_tensor("dmax", [B, 2, NB], F32))
            droot = layer0.enter_context(nc.sbuf_tensor("droot", [B, 2, NB], F32))
            dtmp = layer0.enter_context(nc.sbuf_tensor("dtmp", [B, 2, NB], F32))
            block = scope.enter_context(nc.Block())

            @block.sync
            def _(sp):
                sp.dma_start(deg_rows[:, :], acc[D:D + 1, 0:N].rearrange("o (b p) -> o b p", p=B)).then_inc(t_din, 16)

            @block.tensor
            def _(pe):
                pe.wait_ge(t_din, 16)
                nc.tensor.transpose(pdeg[0:B, 0:NB], deg_rows[:, :], ident[0:NB, 0:NB]).then_inc(t_deg, 1)

            @block.scalar
            def _(act):
                act.wait_ge(t_sq, 1)
                nc.scalar.activation(droot[:, :, :], dmax[:, :, :], ACT.Sqrt).then_inc(t_sq, 1)

            @block.vector
            def _(dve):
                made = [0]

                def link(ins):
                    made[0] += 1
                    ins.then_inc(t_v, 1)
                    dve.wait_ge(t_v, made[0])

                link(nc.vector.tensor_scalar(tile_f[:, 0, :], ends[:, 0, :], -1.0, float(TT), ALU.mult, ALU.add))
                link(nc.vector.tensor_scalar(tile_f[:, 0, :], tile_f[:, 0, :], float(TT - 1), None, ALU.min))
                link(nc.vector.tensor_scalar(tile_f[:, 1, :], ends[:, 1, :], -1.0, 0.0, ALU.add, ALU.max))
                for e in range(2):
                    nc.vector.tensor_copy(tile_i[:, e, :], tile_f[:, e, :])
                dve.wait_ge(t_deg, 1)
                link(nc.vector.tensor_copy(ideg[:, :], pdeg[0:B, 0:NB]))
                for k, deg in enumerate((odeg, ideg)):
                    link(nc.vector.tensor_scalar(dg[:, k, :], deg[:, :], 1.0, None, ALU.min))
                    link(nc.vector.tensor_scalar(dmax[:, k, :], deg[:, :], 1.0, None, ALU.max))
                dve.sem_inc(t_sq, 1)
                dve.wait_ge(t_sq, 2)
                link(nc.vector.reciprocal(droot[:, :, :], droot[:, :, :]))
                link(nc.vector.tensor_tensor(dtmp[:, :, :], droot[:, :, :], droot[:, :, :], ALU.mult))
                link(nc.vector.tensor_tensor(dtmp[:, :, :], dtmp[:, :, :], dmax[:, :, :], ALU.mult))
                link(nc.vector.tensor_scalar(dtmp[:, :, :], dtmp[:, :, :], -0.5, 1.5, ALU.mult, ALU.add))
                link(nc.vector.tensor_tensor(droot[:, :, :], droot[:, :, :], dtmp[:, :, :], ALU.mult))
                link(nc.vector.scalar_tensor_tensor(out=scl[:, :, :], in0=droot[:, :, :], scalar=SCALE, in1=dg[:, :, :],
                                                    op0=ALU.mult, op1=ALU.mult))
                link(nc.vector.tensor_scalar(coef[:, :, :], scl[:, :, :], 0.5 / SCALE / SCALE, None, ALU.mult))
                link(nc.vector.tensor_tensor(bias[0][:, :], bias[0][:, :], bias[1][:, :], ALU.add))
                link(nc.vector.tensor_scalar(bias[0][:, :], bias[0][:, :], 0.5, None, ALU.mult))

        layer0.close()
        edges = whole.enter_context(nc.sbuf_tensor("edges", [P, GC, 2, P], I32))
        near_in = sem("near_in")

        def gather_near(pool):
            for c in range(GC):
                nc.gpsimd.indirect_dma_start(out=edges[:, c, :, :].rearrange("p d e -> p (d e)"), out_offset=None, in_=near[:, :],
                                             in_offset=bass.IndirectOffsetOnAxis(ap=nidx[:, c:c + 1], axis=0)).then_inc(near_in, 16)

        yz = [whole.enter_context(nc.sbuf_tensor(f"yz{k}", [B, NB, 2 * D], F16)) for k in range(2)]
        chunks = [(c, min(4, NB - c)) for c in range(0, NB, 4)]
        with ExitStack() as scope:
            sb, ps = sb_in(scope), ps_in(scope)
            w1 = sb("w1", [D, D], F32)
            b1c = sb("b1c", [D, 1], F32)
            w2 = sb("w2", [D + 1, D], F32)
            CW = 4 * B
            h1 = [sb(f"h1{k}", [D + 1, CW], F32) for k in range(2)]
            norm = norm_buffers(sb, "m")
            wp = sb("wp", [D, 2, D], F32)
            xt = [sb(f"xt{k}", [D, CW], F32) for k in range(2)]
            ts = [sb(f"ts{k}", [B, 2, 4, D], F32) for k in range(4)]
            tile_dst = sb("tile_dst", [P, 2, GC, P], I32)
            hits = sb("hits", [P, GC, P], F32)
            edge = sb("edge", [P, 2, GC], F32)
            reach = sb("reach", [P, 1], F32)
            reach_w = sb("reach_w", [P, P], F32)
            ph_bank = bank(ps, "ph")
            ph = ph_bank[0:D, 0:CW]
            po = [bank(ps, f"po{k}")[0:B, :].rearrange("p (j f) -> p j f", j=4) for k in range(2)]
            pxt = bank(ps, "pxt")[0:D, 0:CW]
            pp = [ps(f"pp{k}", [P, 2, 512], F32)[0:B, :, 0:4 * D].rearrange("p a (j d f) -> p a j d f", j=2, d=2) for k in range(2)]
            s_w, s_h, s_hr, s_o, s_oa, s_v3, s_on, s_hi, s_lo = (sem("m_w"), sem("m_h"), sem("m_hr"), sem("m_o"), sem("m_oa"),
                                                                 sem("m_v"), sem("m_on"), sem("m_hi"), sem("m_lo"))
            s_sq, s_sr, s_nm, s_ap = sem("m_sq"), sem("m_sr"), sem("m_nm"), sem("m_ap")
            s_t, s_xt, s_pp, s_ts = sem("m_t"), sem("m_xt"), sem("m_pp"), sem("m_ts")
            t_in, t_near, t_reach, t_row = [sem(f"t_in{e}") for e in range(2)], sem("t_near"), sem("t_reach"), sem("t_row")
            last_k = len(chunks) - 1
            SEARCH = 2
            block = scope.enter_context(nc.Block())

            @block.sync
            def _(sp):
                sp.dma_start(w1[:, :], w1T).then_inc(s_w, 16)
                sp.dma_start(w2[:, :], w2T).then_inc(s_w, 16)
                sp.dma_start(b1c[:, :], b1).then_inc(s_w, 16)
                sp.dma_start(wp[:, 0, :], wdsT).then_inc(s_w, 16)
                sp.dma_start(wp[:, 1, :], wsdT).then_inc(s_w, 16)
                xb = x.rearrange("(b p) f -> p b f", p=B)
                for b in range(0, NB, X_BLOCKS):
                    sp.dma_start(X[:, b:b + X_BLOCKS, :], xb[:, b:b + X_BLOCKS, :]).then_inc(s_x2[b // X_BLOCKS], 16)
                sp.wait_ge(s_w, 80)

            @block.gpsimd
            def _(pool):
                for e in range(2):
                    for c in range(GC):
                        nc.gpsimd.indirect_dma_start(out=tile_dst[:, e, c, :], out_offset=None, in_=dst_t[:, :],
                                                     in_offset=bass.IndirectOffsetOnAxis(ap=tile_i[:, e, c:c + 1], axis=0)).then_inc(t_in[e], 16)
                for k, (b0, nb) in enumerate(chunks):
                    if k == SEARCH:
                        pool.wait_ge(t_near, 1)
                        gather_near(pool)
                    pool.wait_ge(s_t, k + 1)
                    xb = X[:, b0:b0 + nb, :]
                    nc.gpsimd.tensor_tensor(xb, xb, bias[0][:, :].unsqueeze(1).broadcast_to([B, nb, D]), ALU.add)
                    for d in range(2):
                        pool.wait_ge(s_hi, 2 * k + d + 1)
                        nc.gpsimd.tensor_tensor(yz[d][:, b0:b0 + nb, D:2 * D], ts[k % 4][:, d, 0:nb, :], yz[d][:, b0:b0 + nb, 0:D],
                                                ALU.subtract).then_inc(s_lo, 1)

            @block.tensor
            def _(pe):
                pe.wait_ge(s_w, 80)
                pe.wait_ge(s_on, 2)

                def up_product(k):
                    b0, nb = chunks[k]
                    if k >= 1:
                        pe.wait_ge(s_hr, k)
                    nc.tensor.matmul(ph[:, 0:nb * B], w1[:, :], acc[0:D, b0 * B:(b0 + nb) * B], start=True, stop=True).then_inc(s_h, 1)

                def down_product(k):
                    pe.wait_ge(s_hr, k + 1)
                    if k >= 2:
                        pe.wait_ge(s_oa, k - 1)
                    for j in range(chunks[k][1]):
                        last = nc.tensor.matmul(po[k % 2][:, j, 0:D], h1[k % 2][:, j * B:(j + 1) * B], w2[:, :], start=True, stop=True)
                    last.then_inc(s_o, 1)

                def turn(k):
                    b0, nb = chunks[k]
                    pe.wait_ge(s_ap, k + 1)
                    if k >= 1:
                        pe.wait_ge(s_xt, k)
                    for j in range(nb):
                        last = nc.tensor.transpose(pxt[:, j * B:(j + 1) * B], X[:, b0 + j, :], ident[0:B, 0:B])
                    last.then_inc(s_t, 1)

                def project(k):
                    pe.wait_ge(s_xt, k + 1)
                    if k >= 2:
                        pe.wait_ge(s_ts, 2 * (k - 1))
                    for j in range(chunks[k][1]):
                        last = nc.tensor.matmul(pp[k % 2][:, j // 2, j % 2, :, :], xt[k % 2][:, j * B:(j + 1) * B], wp[:, :, :],
                                                start=True, stop=True)
                    last.then_inc(s_pp, 1)

                up_product(0)
                up_product(1)
                for k in range(len(chunks) + 2):
                    if k <= last_k:
                        down_product(k)
                    if k >= 2:
                        turn(k - 2)
                    if k + 2 <= last_k:
                        up_product(k + 2)
                    if k == last_k:
                        pe.wait_ge(t_reach, 1)
                        pe.wait_ge(s_hr, last_k + 1)
                        nc.tensor.matmul(ph_bank[:, 0:P], reach_w[:, :], ident[:, :], start=True, stop=True).then_inc(t_row, 1)
                    if k >= 2:
                        project(k - 2)

            @block.scalar
            def _(act):
                act.wait_ge(s_w, 80)

                def up_relu(k):
                    nb = chunks[k][1]
                    act.wait_ge(s_h, k + 1)
                    if k >= 2:
                        act.wait_ge(s_o, k - 1)
                    nc.scalar.activation(h1[k % 2][0:D, 0:nb * B], ph[:, 0:nb * B], ACT.Relu, bias=b1c[:, :]).then_inc(s_hr, 1)

                def keep_turned(k):
                    nb = chunks[k][1]
                    act.wait_ge(s_t, k + 1)
                    if k >= 2:
                        act.wait_ge(s_pp, k - 1)
                    nc.scalar.activation(xt[k % 2][:, 0:nb * B], pxt[:, 0:nb * B], ACT.Copy).then_inc(s_xt, 1)

                def high_halves(k):
                    b0, nb = chunks[k]
                    for d in range(2):
                        act.wait_ge(s_ts, 2 * k + d + 1)
                        nc.scalar.activation(yz[d][:, b0:b0 + nb, 0:D], ts[k % 4][:, d, 0:nb, :], ACT.Copy).then_inc(s_hi, 1)

                up_relu(0)
                up_relu(1)
                for k, (b0, nb) in enumerate(chunks):
                    if k >= 2:
                        keep_turned(k - 2)
                    root(nc, act, norm, k, b0, nb, s_sq, s_sr)
                    if k + 2 <= last_k:
                        up_relu(k + 2)
                    if k >= 3:
                        high_halves(k - 3)
                    apply_norm(nc, act, norm, X, k, b0, nb, s_nm, s_ap)
                keep_turned(last_k - 1)
                high_halves(last_k - 2)
                keep_turned(last_k)
                high_halves(last_k - 1)
                high_halves(last_k)

            @block.vector
            def _(dve):
                made = [0]

                def link(ins):
                    made[0] += 1
                    ins.then_inc(s_v3, 1)
                    dve.wait_ge(s_v3, made[0])

                def scaled(k):
                    b0, nb = chunks[k]
                    dve.wait_ge(s_pp, k + 1)
                    if k >= 4:
                        dve.wait_ge(s_lo, 2 * (k - 3))
                    for d in range(2):
                        nc.vector.tensor_tensor(ts[k % 4][:, d, 0:nb, :].rearrange("p (a j) f -> p a j f", j=2), pp[k % 2][:, 0:nb // 2, :, d, :],
                                                scl[:, d, b0:b0 + nb].rearrange("p (a j) -> p a j", j=2).unsqueeze(3).broadcast_to([B, nb // 2, 2, D]),
                                                ALU.mult).then_inc(s_ts, 1)

                def search(part):
                    if part < 2:
                        e, op = part, (ALU.is_ge, ALU.is_le)[part]
                        dve.wait_ge(t_in[e], 16 * GC)
                        link(nc.vector.tensor_tensor(hits[:, :, :], tile_dst[:, e, :, :], thr[:, e, :].unsqueeze(2).broadcast_to([P, GC, P]), op))
                        link(nc.vector.tensor_tensor(hits[:, :, :], hits[:, :, :], ruler[:, e, :].unsqueeze(1).broadcast_to([P, GC, P]), ALU.mult))
                        link(nc.vector.tensor_reduce(edge[:, e, :], hits[:, :, :], AX.X, ALU.max))
                        return
                    link(nc.vector.tensor_scalar(tile_f[:, :, :], tile_f[:, :, :], float(P), None, ALU.mult))
                    link(nc.vector.scalar_tensor_tensor(out=edge[:, 0, :], in0=tile_f[:, 0, :], scalar=float(P), in1=edge[:, 0, :],
                                                        op0=ALU.add, op1=ALU.subtract))
                    link(nc.vector.tensor_tensor(edge[:, 1, :], tile_f[:, 1, :], edge[:, 1, :], ALU.add))
                    link(nc.vector.tensor_copy(nidx[:, :], edge[:, 0, :]))
                    link(nc.vector.tensor_scalar(nidx[:, :], nidx[:, :], STEP.bit_length() - 1, None, ALU.arith_shift_right))
                    link(nc.vector.tensor_scalar(nidx[:, :], nidx[:, :], float(NEAR - 1), None, ALU.min))
                    dve.sem_inc(t_near, 1)
                    link(nc.vector.scalar_tensor_tensor(out=edge[:, 1, :], in0=nidx[:, :], scalar=-float(STEP), in1=edge[:, 1, :],
                                                        op0=ALU.mult, op1=ALU.add))
                    link(nc.vector.tensor_tensor(edge[:, 1, :], edge[:, 1, :], mask[:, :], ALU.mult))
                    link(nc.vector.tensor_reduce(reach[:, :], edge[:, 1, :], AX.X, ALU.max))
                    nc.vector.tensor_scalar(reach_w[:, :], ones[:, :], reach[:, :], None, ALU.mult).then_inc(t_reach, 1)

                for k in range(2):
                    nc.vector.memset(h1[k][D:D + 1, :], 1.0).then_inc(s_on, 1)
                for k, (b0, nb) in enumerate(chunks):
                    dve.wait_ge(s_o, k + 1)
                    dve.wait_ge(s_x2[(b0 + nb - 1) // X_BLOCKS], 16)
                    xb = X[:, b0:b0 + nb, :]
                    nc.vector.tensor_tensor(xb, xb, po[k % 2][:, 0:nb, 0:D], ALU.add).then_inc(s_oa, 1)
                    dve.wait_ge(s_oa, k + 1)
                    statistics(nc, dve, link, norm, X, k, b0, nb, s_sq)
                    if k >= 3:
                        scaled(k - 3)
                    if SEARCH <= k < SEARCH + 3:
                        search(k - SEARCH)
                    inverse_root(nc, dve, link, norm, k, b0, nb, s_sr, s_nm)
                dve.wait_ge(t_row, 1)
                link(nc.vector.tensor_reduce(rnf[:, 1:2], ph_bank[0:1, 0:P], AX.X, ALU.max))
                link(nc.vector.tensor_scalar(rni[:, 1:2], rnf[:, 1:2], float(P - 1), float(P), ALU.add, ALU.max))
                link(nc.vector.tensor_scalar(rounds[:, 1:2], rni[:, 1:2], P.bit_length() - 1, None, ALU.arith_shift_right))
                for k in range(last_k - 2, last_k + 1):
                    scaled(k)

        z, y = yz
        agg = acc[0:B, 0:NB * 2 * D].rearrange("p (b f) -> p b f", b=NB)
        RING = 5
        LEAD = 4
        START = 64
        with ExitStack() as scope:
            sb, ps = sb_in(scope), ps_in(scope)
            T = [sb(f"T{k}", [B, NB, SW], F16) for k in range(2)]
            qn = sb("qn", [P, GC, P], I32)
            keyf = sb("keyf", [P, GC, P], F32)
            lof = sb("lof", [P, GC, P], F32)
            keyt = sb("keyt", [P, GC * P], F16)
            lot = sb("lot", [P, GC * P], F16)
            keys = [sb(f"keys{k}", [P, 2 * PAIRS], F16) for k in range(2)]
            los = [sb(f"los{k}", [P, 2 * PAIRS], F16) for k in range(2)]
            yst = [sb(f"yst{k}", [B, 2, 2 * D], F16) for k in range(2)]
            KO = [sb(f"KO{k}", [P, 2, GW], F16) for k in range(RING)]
            LO = [sb(f"LO{k}", [P, 2, B], F16) for k in range(RING)]
            TX = [sb(f"TX{k}", [B, 2, 2, B], F16) for k in range(2)]
            pt_bank = [bank(ps, f"pt{k}") for k in range(2)]
            pt = [b[0:B, 0:2 * GW].rearrange("p (g n) -> p g n", g=2) for b in pt_bank]
            px = [bank(ps, f"px{k}", F16)[0:B, 0:4 * P].rearrange("p (b h s) -> p b h s", b=2, h=2) for k in range(2)]
            pg = [bank(ps, f"pg{k}") for k in range(2)]
            pl_both = ps("pl", [P, 2, 512], F32)
            pl = [pl_both[:, k, :] for k in range(2)]
            pa = pl_both[0:B, :, 0:2 * D]
            cz = sb("cz", [B, 2, 2 * D], F32)
            g_zero = sem("g_zero")
            g_v = sem("g_v")
            keyed = sem("keyed")
            flipped = sem("flipped")
            tabled = sem("tabled")
            staged = sem("staged")
            y_in = sem("y_in")
            hot = sem("hot")
            pool_hot = sem("pool_hot")
            built = sem("built")
            kept = sem("kept")
            turned = sem("turned")
            held = sem("held")
            summed = sem("summed")
            added = sem("c_added")
            at_done = sem("at_done")
            at_held = sem("at_held")
            at_half = sem("at_half")
            at_kept = sem("at_kept")
            turns = [(b[:, 0:512].rearrange("p (c e) -> p c e", e=P), c, min(4, GC - c), d)
                     for d, banks in enumerate(((pt_bank[0], pt_bank[1], pg[0]), (pl[0], pl[1], pg[1])))
                     for b, c in zip(banks, range(0, GC, 4))]
            assert GC <= 12
            RP = STRIPS * PAIRS
            block = scope.enter_context(nc.Block())

            def done(item):
                return item + (START + 1)

            def before(p):
                return {0: 1, 1: 3}.get(p, 2)

            def count(eng):
                return eng.value_load(rounds[0:1, 1:2], min_val=1, max_val=TT)

            def strips(eng, step):
                step(0, None, 0)
                with eng.Fori(0, (STRIPS - 3) // 2) as k:
                    step(eng.snap(k * 2 + 1), eng.snap(k * 2), 1)
                    step(eng.snap(k * 2 + 2), eng.snap(k * 2 + 1), 0)
                step(STRIPS - 2, STRIPS - 3, 1)
                step(STRIPS - 1, STRIPS - 2, 0)
                step(None, STRIPS - 1, 1)

            @block.gpsimd
            def _(pool):
                pool.sem_inc(y_in, START)
                pool.sem_inc(pool_hot, START)
                nc.gpsimd.memset(agg[:, :, :], 0.0).then_inc(g_zero, 1)
                with pool.Fori(0, count(pool)) as r:
                    def step(b, u, k):
                        if b is None:
                            return
                        b_at = pool.snap(r * RP + b * PAIRS)
                        hold(pool, carrier["pool"], staged, r * (2 * STRIPS) + (b * 2 + 2))
                        for p in range(PAIRS):
                            hold(pool, carrier["pool"], built, done(b_at + (p - RING)))
                            nc.gpsimd.tensor_scalar(LO[p % RING][:, 1, :], iota16[:, :], los[k][:, 2 * p + 1:2 * p + 2],
                                                    None, ALU.is_equal).then_inc(pool_hot, 1)
                            if p == PAIRS // 2:
                                lag = 1 if isinstance(b, int) and b == 0 else 2
                                hold(pool, carrier["pool"], summed, done(r * RP + (b * PAIRS - lag * PAIRS + PAIRS - 1)))
                                nc.gpsimd.tensor_copy(yst[k][:, :, :], y[:, bass.ds(b * 2, 2), :]).then_inc(y_in, 1)
                    strips(pool, step)
                    hold(pool, carrier["pool"], keyed, r + 1)
                    gather_near(pool)
                    hold(pool, carrier["pool"], near_in, r * (16 * GC) + 32 * GC)

            @block.tensor
            def _(pe):
                for s in (built, turned, summed, at_done):
                    pe.sem_inc(s, START)
                with pe.Fori(0, count(pe)) as r:
                    pe.wait_ge(keyed, r + 1)
                    pe.wait_ge(added, done(r * RP - 1))
                    pe.wait_ge(at_held, done(r * STRIPS - 1))
                    pe.wait_ge(kept, done(r * RP - 1))
                    for b, c0, m, d in turns:
                        for c in range(m):
                            last = nc.tensor.transpose(b[:, c, :], (keyf, lof)[d][:, c0 + c, :], ident[:, :])
                        last.then_inc(flipped, 1)
                    pe.wait_ge(tabled, r * len(turns) + len(turns))

                    def step(b, u, k):
                        use = T[1 - k]
                        if b is not None:
                            b_at = pe.snap(r * RP + b * PAIRS)
                        if u is not None:
                            u_at = pe.snap(r * RP + u * PAIRS)
                            pe.wait_ge(kept, done(u_at + (PAIRS - 1)))

                        def sum_slot(p):
                            if p == 0:
                                pe.wait_ge(y_in, done(r * STRIPS + u))
                            pe.wait_ge(held, done(u_at + p))
                            pe.wait_ge(added, done(u_at + (p - before(p))))
                            for h in range(2):
                                for blk in range(2):
                                    last = nc.tensor.matmul(pg[p % 2][0:B, h * 2 * D:(h + 1) * 2 * D], TX[p % 2][:, blk, h, 0:B],
                                                            yst[1 - k][:, blk, :], start=(blk == 0), stop=(blk == 1))
                            last.then_inc(summed, 1)

                        for p in range(PAIRS):
                            if u is not None:
                                pe.wait_ge(held, done(u_at + (p - before(p))))
                                for blk in range(2):
                                    for h in range(2):
                                        last = nc.tensor.transpose(px[p % 2][:, blk, h, 0:B], use[:, 2 * p + h, blk * B:(blk + 1) * B],
                                                                   ident16[0:B, 0:B])
                                last.then_inc(turned, 1)
                            if b is not None:
                                pe.wait_ge(hot, done(b_at + p))
                                pe.wait_ge(pool_hot, done(b_at + p))
                                pe.wait_ge(kept, done(b_at + (p - before(p))))
                                for g in range(2):
                                    last = nc.tensor.matmul(pt[p % 2][:, g, :], LO[p % RING][:, g, :], KO[p % RING][:, g, :],
                                                            start=True, stop=True)
                                last.then_inc(built, 1)
                            if u is not None:
                                if p == 0:
                                    pe.wait_ge(at_held, done(r * STRIPS + u - 1))
                                for h in range(2):
                                    for blk in range(2):
                                        last = nc.tensor.matmul(pa[:, blk, :], use[:, 2 * p + h, blk * B:(blk + 1) * B],
                                                                z[:, 2 * p + h, :], start=(p + h == 0), stop=(p == PAIRS - 1 and h == 1))
                                if p == PAIRS - 1:
                                    last.then_inc(at_done, 1)
                                if p:
                                    sum_slot(p - 1)
                        if u is not None:
                            sum_slot(PAIRS - 1)
                    strips(pe, step)

            @block.scalar
            def _(act):
                act.sem_inc(kept, START)
                act.sem_inc(held, START)
                act.sem_inc(at_held, START)
                with act.Fori(0, count(act)) as r:
                    for n, (b, c0, m, d) in enumerate(turns):
                        act.wait_ge(flipped, r * len(turns) + (n + 1))
                        nc.scalar.activation((keyt, lot)[d][:, c0 * P:(c0 + m) * P].rearrange("p (c e) -> p c e", e=P),
                                             b[:, 0:m, :], ACT.Copy).then_inc(tabled, 1)

                    def step(b, u, k):
                        if b is not None:
                            b_at = act.snap(r * RP + b * PAIRS)
                        if u is not None:
                            u_at = act.snap(r * RP + u * PAIRS)
                        for p in range(PAIRS):
                            if u is not None:
                                act.wait_ge(turned, done(u_at + p))
                                act.wait_ge(summed, done(u_at + (p - before(p))))
                                nc.scalar.activation(TX[p % 2][:, :, :, 0:B], px[p % 2][:, :, :, 0:B], ACT.Copy).then_inc(held, 1)
                            if b is not None:
                                act.wait_ge(built, done(b_at + p))
                                nc.scalar.activation(T[k][:, :, 2 * G * p:2 * G * (p + 1)].rearrange("s h (g d) -> s g h d", g=2),
                                                     pt[p % 2][:, :, :].rearrange("s g (h d) -> s g h d", h=NB), ACT.Copy).then_inc(kept, 1)
                        if u is not None:
                            act.wait_ge(at_done, done(r * STRIPS + u))
                            act.wait_ge(at_kept, done(r * STRIPS + u - 1))
                            nc.scalar.activation(cz[:, :, :], pa, ACT.Copy).then_inc(at_held, 1)
                    strips(act, step)

            @block.vector
            def _(dve):
                for s in (hot, added, at_kept):
                    dve.sem_inc(s, START)
                STEPS = 6
                with dve.Fori(0, count(dve)) as r:
                    v = [0]

                    def link(ins):
                        v[0] += 1
                        ins.then_inc(g_v, 1)
                        dve.wait_ge(g_v, r * STEPS + v[0])

                    dst_e, src_e = edges[:, :, 0, :], edges[:, :, 1, :]
                    dve.wait_ge(near_in, r * (16 * GC) + 16 * GC)
                    nc.vector.tensor_tensor(keyf[:, :, :], dst_e, thr[:, 0, :].unsqueeze(2).broadcast_to([P, GC, P]), ALU.subtract)
                    high(dve, link, src_e, qn[:, :, :])
                    nc.vector.scalar_tensor_tensor(out=lof[:, :, :], in0=qn[:, :, :], scalar=-float(B), in1=src_e, op0=ALU.mult, op1=ALU.add)
                    link(nc.vector.scalar_tensor_tensor(out=keyf[:, :, :], in0=keyf[:, :, :], scalar=float(NB), in1=qn[:, :, :],
                                                        op0=ALU.mult, op1=ALU.add))
                    link(nc.vector.tensor_scalar(keyf[:, :, :], keyf[:, :, :], 1.0, 0.0, ALU.add, ALU.max))
                    link(nc.vector.tensor_scalar(keyf[:, :, :], keyf[:, :, :], float(GW + 1), None, ALU.min))
                    link(nc.vector.tensor_scalar(nidx[:, :], nidx[:, :], float(P // STEP), float(NEAR - 1), ALU.add, ALU.min))
                    dve.sem_inc(keyed, 1)
                    dve.wait_ge(g_zero, 1)
                    hold(dve, carrier["dve"], tabled, r * len(turns) + len(turns))

                    def stage(b, k):
                        for table, strip in ((keyt, keys), (lot, los)):
                            nc.vector.tensor_copy(strip[k][:, :], table[:, bass.ds(b * (2 * PAIRS), 2 * PAIRS)]).then_inc(staged, 1)
                        hold(dve, carrier["dve"], staged, r * (2 * STRIPS) + (b * 2 + 2))

                    def onehots(at, k, p):
                        dve.wait_ge(built, done(at + (p - RING)))
                        for m in range(2):
                            nc.vector.tensor_scalar(KO[p % RING][:, m, :], keytab[:, :], keys[k][:, 2 * p + m:2 * p + m + 1],
                                                    None, ALU.is_equal)
                        nc.vector.tensor_scalar(LO[p % RING][:, 0, :], iota16[:, :], los[k][:, 2 * p:2 * p + 1],
                                                None, ALU.is_equal).then_inc(hot, 1)

                    def step(b, u, k):
                        if b is not None:
                            b_at = dve.snap(r * RP + b * PAIRS)
                        if u is not None:
                            u_at = dve.snap(r * RP + u * PAIRS)
                        first_strip, last_strip = isinstance(b, int) and b == 0, isinstance(b, int) and b == STRIPS - 1
                        if first_strip:
                            stage(b, k)
                            for p in range(LEAD):
                                onehots(b_at, k, p)

                        def add_slot(p):
                            dve.wait_ge(summed, done(u_at + p))
                            dve.wait_ge(added, done(u_at + (p - PAIRS)))
                            a = agg[:, 2 * p:2 * p + 2, :]
                            nc.vector.tensor_tensor(a, a, pg[p % 2][0:B, 0:4 * D].rearrange("p (h f) -> p h f", h=2), ALU.add).then_inc(added, 1)

                        for p in range(PAIRS):
                            if u is not None and p >= 2:
                                add_slot(p - 2)
                            if b is not None and p + LEAD < PAIRS:
                                onehots(b_at, k, p + LEAD)
                            elif b is not None and not last_strip:
                                if p + LEAD == PAIRS:
                                    stage(b + 1, 1 - k)
                                onehots(b_at + PAIRS, 1 - k, p + LEAD - PAIRS)
                        if u is not None:
                            add_slot(PAIRS - 2)
                            add_slot(PAIRS - 1)
                            dve.wait_ge(at_held, done(r * STRIPS + u))
                            dve.wait_ge(at_kept, done(r * STRIPS + u - 1))
                            for part in range(2):
                                for blk in range(2):
                                    a = X[:, bass.ds(u * 2 + blk, 1), :].rearrange("p b f -> p (b f)")
                                    last = nc.vector.scalar_tensor_tensor(out=a, in0=cz[:, blk, part * D:(part + 1) * D], scalar=coef[:, 1, bass.ds(u * 2 + blk, 1)],
                                                                          in1=a, op0=ALU.mult, op1=ALU.add)
                                if part == 0:
                                    last.then_inc(at_half, 1)
                                    hold(dve, carrier["dve"], at_half, r * STRIPS + (u + 1))
                            last.then_inc(at_kept, 1)
                    strips(dve, step)
                    assert v[0] == STEPS, v

        with ExitStack() as scope:
            sb, ps = sb_in(scope), ps_in(scope)
            wide_chunks = [(c, min(8, NB - c)) for c in range(0, NB, 8)]
            norm = norm_buffers(sb, "f")
            f_h, f_a, f_v, f_out = sem("f_h"), sem("f_a"), sem("f_v"), sem("f_out")
            f_sq, f_sr, f_nm, f_ap = sem("f_sq"), sem("f_sr"), sem("f_nm"), sem("f_ap")
            block = scope.enter_context(nc.Block())

            @block.sync
            def _(sp):
                ob = out.rearrange("(b p) f -> p b f", p=B)
                for k, (b0, nb) in enumerate(wide_chunks):
                    sp.wait_ge(f_ap, k + 1)
                    sp.dma_start(ob[:, b0:b0 + nb, :], X[:, b0:b0 + nb, :]).then_inc(f_out, 16)
                sp.wait_ge(f_out, 16 * len(wide_chunks))

            @block.gpsimd
            def _(pool):
                for b0, nb in wide_chunks:
                    a = agg[:, b0:b0 + nb, 0:D]
                    nc.gpsimd.tensor_tensor(a, a, agg[:, b0:b0 + nb, D:2 * D], ALU.add).then_inc(f_h, 1)

            @block.scalar
            def _(act):
                for k, (b0, nb) in enumerate(wide_chunks):
                    root(nc, act, norm, k, b0, nb, f_sq, f_sr)
                    apply_norm(nc, act, norm, X, k, b0, nb, f_nm, f_ap)

            @block.vector
            def _(dve):
                made = [0]

                def link(ins):
                    made[0] += 1
                    ins.then_inc(f_v, 1)
                    dve.wait_ge(f_v, made[0])

                for k, (b0, nb) in enumerate(wide_chunks):
                    dve.wait_ge(f_h, k + 1)
                    for b in range(b0, b0 + nb):
                        last = nc.vector.scalar_tensor_tensor(out=X[:, b, :], in0=agg[:, b, 0:D], scalar=coef[:, 0, b:b + 1],
                                                              in1=X[:, b, :], op0=ALU.mult, op1=ALU.add)
                    last.then_inc(f_a, 1)
                    dve.wait_ge(f_a, k + 1)
                    statistics(nc, dve, link, norm, X, k, b0, nb, f_sq)
                    if k:
                        b1_, nb1 = wide_chunks[k - 1]
                        inverse_root(nc, dve, link, norm, k - 1, b1_, nb1, f_sr, f_nm)
                inverse_root(nc, dve, link, norm, len(wide_chunks) - 1, *wide_chunks[-1], f_sr, f_nm)


def kernel(x, src, dst, edge_attr_96, L0_gnn_W_edge, L0_gnn_b_edge, L0_gnn_eps, L0_gnn_W1, L0_gnn_b1, L0_gnn_W2, L0_gnn_b2,
           L1_gnn_W_sd, L1_gnn_b_sd, L1_gnn_W_ds, L1_gnn_b_ds):
    import numpy as np
    import concourse.bacc as bacc
    from concourse.bass_utils import run_bass_kernel_spmd

    def padded(a, fill, n):
        out = np.full((n,), fill, np.int32)
        out[:E] = np.asarray(a)
        return out

    def rows_near(a):
        return np.lib.stride_tricks.sliding_window_view(padded(a, N, TT * P), P)[::STEP]

    def by_edge(a):
        return np.ascontiguousarray(padded(a, N, TILES * P).reshape(TILES, P).T)

    def with_bias(w, b):
        return np.ascontiguousarray(np.concatenate([np.asarray(w).T, np.asarray(b)[None, :]], axis=0))

    x = np.ascontiguousarray(x)
    ea = np.zeros((D, TILES * P), np.float32)
    ea[:, :E] = np.asarray(edge_attr_96).T
    arrays = {
        "x": x,
        "xT": np.ascontiguousarray(x.T),
        "dst_t": padded(dst, N, TT * P).reshape(TT, P),
        "near": np.concatenate([rows_near(dst), rows_near(src)], axis=1),
        "dst_et": by_edge(dst), "src_et": by_edge(src),
        "src_gather": np.ascontiguousarray(padded(src, 0, TILES * P).reshape(2 * CH, HT, P).transpose(0, 2, 1)),
        "eaT": ea,
        "weT": with_bias(L0_gnn_W_edge, L0_gnn_b_edge),
        "w1T": np.ascontiguousarray(np.asarray(L0_gnn_W1).T),
        "b1": np.ascontiguousarray(L0_gnn_b1).reshape(D, 1),
        "w2T": with_bias(L0_gnn_W2, L0_gnn_b2),
        "eps": np.ascontiguousarray(L0_gnn_eps).reshape(1, 1),
        "wsdT": np.ascontiguousarray(np.asarray(L1_gnn_W_sd).T),
        "wdsT": np.ascontiguousarray(np.asarray(L1_gnn_W_ds).T),
        "bsd": np.ascontiguousarray(L1_gnn_b_sd).reshape(1, D),
        "bds": np.ascontiguousarray(L1_gnn_b_ds).reshape(1, D),
    }
    nc = bacc.Bacc("TRN2", target_bir_lowering=False, num_devices=1)
    args = [nc.dram_tensor("in_" + k, a.shape, mybir.dt.from_np(a.dtype), kind="ExternalInput").ap() for k, a in arrays.items()]
    out = nc.dram_tensor("out", (N, D), F32, kind="ExternalOutput").ap()
    gnn(nc, *args, out)
    result = run_bass_kernel_spmd(nc, [{"in_" + k: a for k, a in arrays.items()}], core_ids=[0])
    return result.results[0]["out"]
```
